# Optimizing a Trainium2 kernel written in Bass

```python
import numpy as np
import jax
import jax.numpy as jnp

def _softmax(x, axis=-1):
    return jax.nn.softmax(x, axis=axis)

def _gelu(x):
    return jax.nn.gelu(x, approximate=True)

def _silu(x):
    return jax.nn.silu(x)

def _sigmoid(x):
    return jax.nn.sigmoid(x)

def _layernorm(x, axis=-1, eps=1e-05):
    m = jnp.mean(x, axis=axis, keepdims=True)
    v = jnp.var(x, axis=axis, keepdims=True)
    return (x - m) / jnp.sqrt(v + eps)

def _scatter_add(tgt, idx, src, axis=0):
    return tgt.at[idx].add(src)

def _segment_sum(src, seg, n):
    return jax.ops.segment_sum(src, seg, n)
kernel_name = 'mk_gnn_resnorm_d1_gnn_r32_957e03'

def setup_inputs(seed: int=0):
    np.random.seed(seed)
    _w = jnp.asarray

    def _rec_inputs():
        import jax
        import jax.numpy as jnp
        _gk = jax.random.key(seed)
        x = -0.000202 + 1 * jax.random.normal(jax.random.fold_in(_gk, 1), (50000, 128), jnp.float32)
        src = jax.random.randint(jax.random.fold_in(_gk, 2), (50000,), 0, 50000, jnp.int32)
        dst = jnp.minimum((50000 * jax.random.uniform(jax.random.fold_in(_gk, 3), (50000,)) ** 2.0).astype(jnp.int32), 49999)
        _o = jnp.argsort(dst, stable=True)
        src = src[_o]
        dst = dst[_o]
        edge_weight = jax.random.uniform(jax.random.fold_in(_gk, 12), (50000,), jnp.float32, 0.0, 0.999998)
        return (x, src, dst, edge_weight)
    x, src, dst, edge_weight = _rec_inputs()

    def _L0_gnn_setup():
        import jax, jax.numpy as jnp
        import numpy as np
        N, E, H = (50000, 25000, 128)
        LN_EPS = 1e-05

        def layer_norm(x, gamma, beta):
            mu = jnp.mean(x, axis=-1, keepdims=True)
            var = jnp.mean((x - mu) ** 2, axis=-1, keepdims=True)
            return (x - mu) * jax.lax.rsqrt(var + LN_EPS) * gamma + beta
        key = jax.random.key(seed)
        ks = jax.random.split(key, 8)
        sc = 1.0 / np.sqrt(2 * H)
        return {'x': jax.random.normal(ks[0], (N, H), dtype=jnp.float32), 'edge_index': jax.random.randint(ks[1], (2, E), 0, N, dtype=jnp.int64), 'edge_weights': jax.random.uniform(ks[2], (E,), dtype=jnp.float32), 'msg_w': jax.random.normal(ks[3], (2 * H, H), dtype=jnp.float32) * sc, 'msg_b': jnp.zeros((H,), jnp.float32), 'msg_g': jnp.ones((H,), jnp.float32), 'msg_beta': jnp.zeros((H,), jnp.float32), 'upd_w': jax.random.normal(ks[4], (2 * H, H), dtype=jnp.float32) * sc, 'upd_b': jnp.zeros((H,), jnp.float32), 'upd_g': jnp.ones((H,), jnp.float32), 'upd_beta': jnp.zeros((H,), jnp.float32), 'gate_w': jax.random.normal(ks[5], (H, 1), dtype=jnp.float32) / np.sqrt(H), 'gate_b': jnp.zeros((1,), jnp.float32)}
    _L0_gnn_all = _L0_gnn_setup()
    _L0_gnn_in = {k: v for k, v in _L0_gnn_all.items() if k in ('msg_w', 'msg_b', 'msg_g', 'msg_beta', 'upd_w', 'upd_b', 'upd_g', 'upd_beta', 'gate_w', 'gate_b')}
    del _L0_gnn_all
    return {'x': x, 'src': src, 'dst': dst, 'edge_weight': edge_weight, 'L0_gnn_msg_w': _L0_gnn_in['msg_w'], 'L0_gnn_msg_b': _L0_gnn_in['msg_b'], 'L0_gnn_msg_g': _L0_gnn_in['msg_g'], 'L0_gnn_msg_beta': _L0_gnn_in['msg_beta'], 'L0_gnn_upd_w': _L0_gnn_in['upd_w'], 'L0_gnn_upd_b': _L0_gnn_in['upd_b'], 'L0_gnn_upd_g': _L0_gnn_in['upd_g'], 'L0_gnn_upd_beta': _L0_gnn_in['upd_beta'], 'L0_gnn_gate_w': _L0_gnn_in['gate_w'], 'L0_gnn_gate_b': _L0_gnn_in['gate_b']}

def reference(x, src, dst, edge_weight, L0_gnn_msg_w, L0_gnn_msg_b, L0_gnn_msg_g, L0_gnn_msg_beta, L0_gnn_upd_w, L0_gnn_upd_b, L0_gnn_upd_g, L0_gnn_upd_beta, L0_gnn_gate_w, L0_gnn_gate_b):
    import jax
    import jax.numpy as jnp

    def _L0_gnn_ref(x, edge_index, edge_weights, msg_w, msg_b, msg_g, msg_beta, upd_w, upd_b, upd_g, upd_beta, gate_w, gate_b):
        import jax, jax.numpy as jnp
        import numpy as np
        N, E, H = (50000, 25000, 128)
        LN_EPS = 1e-05

        def layer_norm(x, gamma, beta):
            mu = jnp.mean(x, axis=-1, keepdims=True)
            var = jnp.mean((x - mu) ** 2, axis=-1, keepdims=True)
            return (x - mu) * jax.lax.rsqrt(var + LN_EPS) * gamma + beta
        num_nodes = x.shape[0]
        src, dst = (edge_index[0], edge_index[1])
        em = jnp.concatenate([x[src], x[dst]], axis=-1)
        em = jax.nn.relu(layer_norm(em @ msg_w + msg_b, msg_g, msg_beta))
        em = em * edge_weights[:, None]
        msgs = jax.ops.segment_sum(em, dst, num_segments=num_nodes)
        counts = jax.ops.segment_sum(jnp.ones((src.shape[0], 1), x.dtype), dst, num_segments=num_nodes)
        valid = (counts > 0).astype(x.dtype)
        messages = msgs / (counts + 1e-08) * valid
        gate = jax.nn.sigmoid(x @ gate_w + gate_b)
        combined = jnp.concatenate([x, messages], axis=-1)
        h_new = jax.nn.relu(layer_norm(combined @ upd_w + upd_b, upd_g, upd_beta))
        return gate * h_new + (1.0 - gate) * x
    edge_index = jnp.stack([src, dst])
    x = _layernorm(x + _L0_gnn_ref(x, edge_index, edge_weight, L0_gnn_msg_w, L0_gnn_msg_b, L0_gnn_msg_g, L0_gnn_msg_beta, L0_gnn_upd_w, L0_gnn_upd_b, L0_gnn_upd_g, L0_gnn_upd_beta, L0_gnn_gate_w, L0_gnn_gate_b), axis=-1)
    return x

_drawn_inputs = setup_inputs


def setup_inputs(seed=0):
    import zlib

    import numpy as np

    out = dict(_drawn_inputs(seed))
    spreads = {'L0_gnn_msg_b': (0.0, 0.8),
     'L0_gnn_msg_g': (1.0, 0.6),
     'L0_gnn_msg_beta': (0.0, 0.8),
     'L0_gnn_upd_b': (0.0, 0.1),
     'L0_gnn_upd_g': (1.0, 0.2),
     'L0_gnn_upd_beta': (0.0, 0.297)}
    factors = {}
    for name, (base, spread) in spreads.items():
        noise = np.random.default_rng([zlib.crc32(name.encode()), seed]).standard_normal(out[name].shape)
        drawn = base * np.exp(spread * noise) if base else spread * noise
        out[name] = jnp.asarray(drawn.astype(out[name].dtype))
    for name, factor in factors.items():
        out[name] = (out[name] * factor).astype(out[name].dtype)
    return out
```

```python
import numpy as np
import concourse.bass as bass
from concourse import mybir
from contextlib import ExitStack

P = 128
F32 = mybir.dt.float32
BF16 = mybir.dt.bfloat16
I32 = mybir.dt.int32
ALU = mybir.AluOpType
ACT = mybir.ActivationFunctionType
AX = mybir.AxisListType
EPS = 1e-5
COUNT_EPS = 1e-8


def build(nc, x, src, dst, edge_w, msg_w, msg_b, msg_g, msg_beta, upd_w, upd_b, upd_g, upd_beta, gate_w, gate_b, out):
    N, H = x.shape
    E = src.shape[0]
    assert H == P
    BODY = 8
    PAIRS = BODY // 2
    BODIES = -(-E // (P * BODY))
    TILES = BODIES * BODY
    FULL = E // TILES
    REST = E - FULL * TILES
    LAG = 6
    ROW = H + 1
    TROWS = P * TILES
    assert TROWS >= N + P and FULL == P - 1
    LATER = 1.0 / 1024
    ZC = 8
    ZROWS = TILES // ZC
    GT = 8
    GN = GT * P
    GROUPS = -(-N // GN)
    GLAST = N - GN

    table = nc.dram_tensor("table", [TROWS, ROW], F32).ap()

    ctx = ExitStack()
    with ctx:
        def sb(name, shape, dt=F32):
            return ctx.enter_context(nc.sbuf_tensor(name, shape, dt))

        def sem(name):
            return ctx.enter_context(nc.semaphore(name))

        ident = sb("ident", [P, P])
        order = sb("order", [P, P])
        ones3 = sb("ones3", [3, P], BF16)
        zeros = sb("zeros", [P, ZROWS * ROW])
        eps_c = sb("eps_c", [P, 1])
        zero_c = sb("zero_c", [P, 1])
        spare_row = sb("spare_row", [P, 1])
        msg_raw = sb("msg_raw", [P, 2, H])
        msg_wg = sb("msg_wg", [P, 2, 2 * H])
        upd_raw = sb("upd_raw", [P, 2, H])
        upd_c = sb("upd_c", [P, 2, H + 1])
        neg_mean = sb("neg_mean", [P, 6])
        gains = sb("gains", [P, 2, H])
        betas = sb("betas", [P, 2, H])
        bias_raw = sb("bias_raw", [1, 2, H])
        bias_m = sb("bias_m", [1, 2 * H])
        bias_u = sb("bias_u", [1, H + 1])
        part_m = sb("part_m", [1, 3, 2 * H], BF16)
        part_u = sb("part_u", [1, 3, H + 1], BF16)
        bias3_m = sb("bias3_m", [3, 2 * H], BF16)
        bias3_u = sb("bias3_u", [3, H + 1], BF16)
        src_t = sb("src_t", [P, TILES + BODY], I32)
        dst_t = sb("dst_t", [P, TILES + BODY], I32)
        w_t = sb("w_t", [P, TILES + BODY])
        key_t = sb("key_t", [P, TILES + BODY])
        above_t = sb("above_t", [P, TILES + BODY])
        dgat_t = sb("dgat_t", [P, TILES + BODY])
        src_i = sb("src_i", [P, BODY], I32)
        dst_i = sb("dst_i", [P, BODY], I32)
        key_s = sb("key_s", [P, BODY])
        above_s = sb("above_s", [P, BODY])
        w_s = sb("w_s", [P, BODY])
        rows = sb("rows", [P, BODY, 2, H])
        xT = sb("xT", [P, 2, 4 * P])
        same = sb("same", [P, 4, P])
        dup = sb("dup", [P, BODY])
        pick = sb("pick", [P, BODY])
        scat_i = sb("scat_i", [P, BODY], I32)
        sumsq = sb("sumsq", [P, BODY])
        std = sb("std", [P, BODY])
        rstd = sb("rstd", [P, BODY])
        junk = sb("junk", [P, 2, P])
        z = sb("z", [P, 4, P])
        em = sb("em", [P, 4, P])
        stage = sb("stage", [P, BODY, ROW])
        xg = sb("xg", [P, 2, GT, H])
        tg = sb("tg", [P, 2, GT, ROW])
        cnt = sb("cnt", [P, 2, 3, GT])
        mg = sb("mg", [P, 2, GT, H])
        yn = sb("yn", [P, 2, GT, H])
        nbuf = sb("nbuf", [P, GT, H])
        og = sb("og", [P, 2, GT, H])
        nss = sb("nss", [P, GT])
        nln = sb("nln", [P, GT])
        nr = sb("nr", [P, GT])
        gexp = sb("gexp", [P, GT])
        gden = sb("gden", [P, GT])
        gate = sb("gate", [P, GT])
        keep = sb("keep", [P, GT])
        stats = sb("stats", [P, GT, 6])
        mv = sb("mv", [P, GT, 2])
        oln = sb("oln", [P, GT])
        orr = sb("orr", [P, 2, GT])
        osh = sb("osh", [P, 2, GT])

        bank = [ctx.enter_context(nc.psum_tensor(f"bank{i}", [P, 512], F32)) for i in range(8)]
        XTb, Yb, Db, Ab = bank[0:2], bank[2:4], bank[4:6], bank[6:8]
        YN = [bank[2], bank[3], bank[4], bank[5]]

        loaded_idx = sem("loaded_idx")
        loaded_w = sem("loaded_w")
        filled = sem("filled")
        setup_step = sem("setup_step")
        zeroed = sem("zeroed")
        consts = sem("consts")
        setup = sem("setup")
        parts_ready = sem("parts_ready")
        bias_placed = sem("bias_placed")
        idx_staged = sem("idx_staged")
        key_staged = sem("key_staged")
        gathered = [sem(f"gathered{u}") for u in range(BODY)]
        transposed = sem("transposed")
        xT_ready = sem("xT_ready")
        y_ready = sem("y_ready")
        squared = sem("squared")
        std_ready = sem("std_ready")
        same_made = sem("same_made")
        picked = sem("picked")
        scat_ready = sem("scat_ready")
        rstd_made = sem("rstd_made")
        z_made = sem("z_made")
        em_made = sem("em_made")
        summed = sem("summed")
        staged = sem("staged")
        scattered = sem("scattered")
        node_loaded = [sem(f"node_loaded{i}") for i in range(2)]
        cnt_a = sem("cnt_a")
        scale_ready = sem("scale_ready")
        mean_made = sem("mean_made")
        n_transposed = sem("n_transposed")
        n_xT = sem("n_xT")
        n_y = sem("n_y")
        n_squared = sem("n_squared")
        n_ln = sem("n_ln")
        n_rstd = sem("n_rstd")
        n_small = sem("n_small")
        n_gate = sem("n_gate")
        n_z = sem("n_z")
        n_shift = sem("n_shift")
        n_h = sem("n_h")
        n_out_y = sem("n_out_y")
        n_stats = sem("n_stats")
        n_mv = sem("n_mv")
        o_ln = sem("o_ln")
        o_r = sem("o_r")
        o_shift = sem("o_shift")
        o_done = sem("o_done")
        stored = [sem(f"stored{i}") for i in range(2)]

        block = ctx.enter_context(nc.Block())

        def await_next(eng, sem, count, by):
            eng.wait_ge(sem, count)
            eng.reg_add(count, count, by)

        def bodies(eng, body):
            body(0, True)
            with eng.Fori(1, BODIES) as i:
                body(i, False)

        def groups(eng, group):
            group(0, 0, True)
            group(1, 1, True)
            with eng.Fori(1, GROUPS // 2) as h:
                group(2 * h, 0, False)
                group(2 * h + 1, 1, False)
            group(GROUPS - 1, 0, False)

        assert GROUPS % 2 == 1

        @block.sync
        def _(sp):
            sp.wait_ge(filled, 4)
            for t, a in ((src_t, src), (dst_t, dst)):
                sp.dma_start(t[0:FULL, 0:TILES], a[0:FULL * TILES].rearrange("(p t) -> p t", t=TILES)).then_inc(loaded_idx, 16)
                sp.dma_start(t[FULL:P, 0:REST], a[FULL * TILES:E].rearrange("(a t) -> a t", a=1)).then_inc(loaded_idx, 16)
            sp.dma_start(w_t[0:FULL, 0:TILES], edge_w[0:FULL * TILES].rearrange("(p t) -> p t", t=TILES)).then_inc(loaded_w, 16)
            sp.dma_start(w_t[FULL:P, 0:REST], edge_w[FULL * TILES:E].rearrange("(a t) -> a t", a=1)).then_inc(loaded_w, 16)
            sp.dma_start(msg_raw[:, :, :], msg_w.rearrange("(a p) n -> p a n", p=P)).then_inc(loaded_w, 16)
            sp.dma_start(upd_raw[:, :, :], upd_w.rearrange("(a p) n -> p a n", p=P)).then_inc(loaded_w, 16)
            sp.dma_start(upd_c[:, 0, H:H + 1], gate_w).then_inc(loaded_w, 16)
            for j, (g, b) in enumerate(((msg_g, msg_beta), (upd_g, upd_beta))):
                sp.dma_start(gains[:, j, :], g.rearrange("(a n) -> a n", a=1).broadcast_to([P, H])).then_inc(loaded_w, 16)
                sp.dma_start(betas[:, j, :], b.rearrange("(a n) -> a n", a=1).broadcast_to([P, H])).then_inc(loaded_w, 16)
            sp.dma_start(bias_raw[:, 0, :], msg_b.rearrange("(a n) -> a n", a=1)).then_inc(loaded_w, 16)
            sp.dma_start(bias_raw[:, 1, :], upd_b.rearrange("(a n) -> a n", a=1)).then_inc(loaded_w, 16)
            sp.dma_start(bias_u[:, H:H + 1], gate_b.rearrange("(a n) -> a n", a=1)).then_inc(loaded_w, 16)
            zview = table.rearrange("(p c r) n -> p c (r n)", c=ZC, r=ZROWS)
            for c in range(ZC):
                sp.dma_start(zview[:, c, :], zeros[:, :]).then_inc(zeroed, 16)
            sp.wait_ge(parts_ready, 6)
            for j in range(3):
                sp.dma_start(bias3_m[j:j + 1, :], part_m[:, j, :]).then_inc(bias_placed, 16)
                sp.dma_start(bias3_u[j:j + 1, :], part_u[:, j, :]).then_inc(bias_placed, 16)

            sp.wait_ge(scattered, 16 * TILES)

            def load(g, s, first):
                base = GLAST if isinstance(g, int) and g == GROUPS - 1 else g * GN
                if not first:
                    sp.wait_ge(n_out_y, PAIRS * (g - 1))
                sp.dma_start(xg[:, s, :, :].rearrange("p t n -> p (t n)"),
                             x[bass.ds(base, GN), :].rearrange("(p t) n -> p (t n)", t=GT)).then_inc(node_loaded[s], 16)
                sp.dma_start(tg[:, s, :, :].rearrange("p t n -> p (t n)"),
                             table[bass.ds(base, GN), :].rearrange("(p t) n -> p (t n)", t=GT)).then_inc(node_loaded[s], 16)
            groups(sp, load)

        @block.gpsimd
        def _(pool):
            slot_used = pool.alloc_register("slot_used")
            before = pool.alloc_register("before")
            pool.reg_mov(slot_used, 1)
            pool.reg_mov(before, 16)
            nc.gpsimd.memset(src_t[:, :], 0).then_inc(filled, 1)
            nc.gpsimd.memset(dst_t[:, :], N + P - 1).then_inc(filled, 1)
            nc.gpsimd.memset(w_t[:, :], 0.0).then_inc(filled, 1)
            nc.gpsimd.memset(ident[:, :], 0.0).then_inc(consts, 1)
            nc.gpsimd.memset(order[:, :], 1.0).then_inc(consts, 1)
            pool.wait_ge(consts, 2)
            nc.gpsimd.affine_select(out=ident[:, :], in_=ident[:, :], compare_op=ALU.not_equal, fill=1.0,
                                    base=0, pattern=[[-1, P]], channel_multiplier=1).then_inc(consts, 1)
            nc.gpsimd.affine_select(out=order[:, :], in_=order[:, :], compare_op=ALU.is_ge, fill=LATER,
                                    base=0, pattern=[[1, P]], channel_multiplier=-1).then_inc(consts, 1)
            nc.gpsimd.iota(spare_row[:, :], pattern=[[0, 1]], base=N, channel_multiplier=1,
                           allow_small_or_imprecise_dtypes=True).then_inc(consts, 1)

            def gather(t, u, first):
                if u % 4 == 0:
                    pool.wait_ge(idx_staged, 2 * t + u // 4 + 1)
                if not first:
                    await_next(pool, transposed, slot_used, 1)
                for j, idx in ((0, src_i), (1, dst_i)):
                    nc.gpsimd.indirect_dma_start(
                        rows[:, u, j, :], None, x, bass.IndirectOffsetOnAxis(ap=idx[:, u:u + 1], axis=0)
                    ).then_inc(gathered[u], 16)

            def scatter(i, u):
                pool.wait_ge(staged, PAIRS * i + (u // 2 + 1))
                pool.wait_ge(scat_ready, 2 * (PAIRS * i + (u // 2 + 1)))
                if isinstance(i, int) and i == 0 and u == 0:
                    pool.wait_ge(zeroed, 16 * ZC)
                else:
                    await_next(pool, scattered, before, 16)
                nc.gpsimd.indirect_dma_start(
                    table, bass.IndirectOffsetOnAxis(ap=scat_i[:, u:u + 1], axis=0), stage[:, u, :], None,
                    compute_op=ALU.add).then_inc(scattered, 16)

            def body(i, first):
                for u in range(BODY):
                    if u >= LAG:
                        scatter(i, u - LAG)
                    elif not first:
                        scatter(i - 1, u - LAG + BODY)
                    gather(i, u, first)
            bodies(pool, body)
            for u in range(BODY - LAG, BODY):
                scatter(BODIES - 1, u)

            def group(g, s, first):
                pool.wait_ge(scale_ready, g + 1)
                if not first:
                    pool.wait_ge(n_transposed, PAIRS * (g - 1))
                nc.gpsimd.tensor_tensor(mg[:, s, :, :], tg[:, s, :, 0:H],
                                        cnt[:, s, 2, :].unsqueeze(2).broadcast_to([P, GT, H]), ALU.mult).then_inc(mean_made, 1)
            groups(pool, group)

        @block.tensor
        def _(pe):
            pe.wait_ge(consts, 5)
            pe.wait_ge(bias_placed, 96)
            pe.wait_ge(setup, 1)

            def products(i, k):
                s = PAIRS * i + k
                b = k % 2
                if k == 0:
                    pe.wait_ge(key_staged, i + 1)
                for h in range(2):
                    u = 2 * k + h
                    nc.tensor.transpose(Db[b][:, h * P:(h + 1) * P], key_s[:, u:u + 1].broadcast_to([P, P]), ident[:, :])
                for h in range(2):
                    u = 2 * k + h
                    pe.wait_ge(gathered[u], 32 * i + 32)
                    for j in range(2):
                        last = nc.tensor.transpose(XTb[b][:, (2 * h + j) * P:(2 * h + j + 1) * P], rows[:, u, j, :], ident[:, :])
                    last.then_inc(transposed, 1)
                pe.wait_ge(xT_ready, s + 1)
                for h in range(2):
                    o = Yb[b][:, h * 2 * H:(h + 1) * 2 * H]
                    nc.tensor.matmul(o, ones3[:, :], bias3_m[:, :], start=True, stop=False)
                    nc.tensor.matmul(o, xT[:, b, 2 * h * P:(2 * h + 1) * P], msg_wg[:, 0, :], start=False, stop=False)
                    last = nc.tensor.matmul(o, xT[:, b, (2 * h + 1) * P:(2 * h + 2) * P], msg_wg[:, 1, :], start=False, stop=True)
                last.then_inc(y_ready, 1)

            def sums(s, b, early):
                pe.wait_ge(em_made, 2 * s + 2)
                if not early:
                    pe.wait_ge(staged, s - 1)
                for h in range(2):
                    q = 2 * b + h
                    last = nc.tensor.matmul(Ab[b][:, h * P:(h + 1) * P], same[:, q, :], em[:, q, :], start=True, stop=True)
                last.then_inc(summed, 1)

            def body(i, first):
                for k in range(PAIRS):
                    products(i, k)
                    if not (first and k == 0):
                        sums(PAIRS * i + (k - 1), (k - 1) % 2, first and k <= 2)
            bodies(pe, body)
            sums(PAIRS * BODIES - 1, 1, False)

            pe.wait_ge(staged, PAIRS * BODIES)

            def group(g, s, first):
                pe.wait_ge(node_loaded[s], (g // 2 + 1) * 32 if isinstance(g, int) else 16 * g + (32 - 16 * s))
                pe.wait_ge(mean_made, g + 1)
                for k in range(PAIRS):
                    r = PAIRS * g + k
                    b = k % 2
                    if not (first and s == 0 and k < 2):
                        pe.wait_ge(n_xT, r - 1)
                    for h in range(2):
                        t = 2 * k + h
                        nc.tensor.transpose(XTb[b][:, 2 * h * P:(2 * h + 1) * P], xg[:, s, t, :], ident[:, :])
                        last = nc.tensor.transpose(XTb[b][:, (2 * h + 1) * P:(2 * h + 2) * P], mg[:, s, t, :], ident[:, :])
                    last.then_inc(n_transposed, 1)
                    pe.wait_ge(n_xT, r + 1)
                    if not (first and s == 0):
                        pe.wait_ge(n_z, r - (PAIRS - 1))
                    for h in range(2):
                        o = YN[k][:, h * (H + 1):(h + 1) * (H + 1)]
                        nc.tensor.matmul(o, ones3[:, :], bias3_u[:, :], start=True, stop=False)
                        nc.tensor.matmul(o, xT[:, b, 2 * h * P:(2 * h + 1) * P], upd_c[:, 0, :], start=False, stop=False)
                        last = nc.tensor.matmul(o, xT[:, b, (2 * h + 1) * P:(2 * h + 2) * P], upd_c[:, 1, :], start=False, stop=True)
                    last.then_inc(n_y, 1)
            groups(pe, group)

        @block.scalar
        def _(act):
            act.wait_ge(setup, 1)

            def products(i, k, first):
                s = PAIRS * i + k
                b = k % 2
                act.wait_ge(transposed, 2 * s + 2)
                if not (first and k < 2):
                    act.wait_ge(y_ready, s - 1)
                nc.scalar.activation(xT[:, b, :], XTb[b][:, :], ACT.Copy).then_inc(xT_ready, 1)
                act.wait_ge(y_ready, s + 1)
                for h in range(2):
                    u = 2 * k + h
                    if h == 0 and not (first and k == 0):
                        act.wait_ge(squared, 2 * s)
                    nc.scalar.activation(junk[:, h, :], Yb[b][:, h * 2 * H:h * 2 * H + H], ACT.Square, bias=zero_c[:, :],
                                         accum_out=sumsq[:, u:u + 1]).then_inc(squared, 1)
                act.wait_ge(squared, 2 * s + 2)
                nc.scalar.activation(std[:, 2 * k:2 * k + 2], sumsq[:, 2 * k:2 * k + 2], ACT.Sqrt, bias=eps_c[:, :],
                                     scale=1.0 / H).then_inc(std_ready, 1)

            def sums(s, k, no_scatter):
                b = k % 2
                act.wait_ge(summed, s + 1)
                if not no_scatter:
                    act.wait_ge(scattered, 32 * s + 16 * (2 - BODY))
                nc.scalar.activation(stage[:, 2 * k:2 * k + 2, 0:H], Ab[b][:, 0:2 * P].rearrange("p (h n) -> p h n", h=2),
                                     ACT.Copy).then_inc(staged, 1)

            def body(i, first):
                for k in range(PAIRS):
                    products(i, k, first)
                    if not (first and k == 0):
                        sums(PAIRS * i + (k - 1), (k - 1) % PAIRS, first)
            body(0, True)
            with act.Fori(1, BODIES) as i:
                body(i, False)
            sums(PAIRS * BODIES - 1, PAIRS - 1, False)

            def finish(g, s, first):
                act.wait_ge(o_shift, g + 1)
                if not first:
                    act.wait_ge(stored[s], (g // 2) * 16 if isinstance(g, int) else 8 * g - 8 * s)
                for t in range(GT):
                    last = nc.scalar.activation(og[:, s, t, :], yn[:, s, t, :], ACT.Identity, scale=orr[:, s, t:t + 1],
                                                bias=osh[:, s, t:t + 1])
                last.then_inc(o_done, 1)
                act.wait_ge(o_done, g + 1)
                base = g * GN
                if isinstance(g, int) and g == GROUPS - 1:
                    base = GLAST
                    act.wait_ge(stored[1], (GROUPS // 2) * 16)
                act.dma_start(out[bass.ds(base, GN), :].rearrange("(p t) n -> p (t n)", t=GT),
                              og[:, s, :, :].rearrange("p t n -> p (t n)")).then_inc(stored[s], 16)

            def group(g, s, first):
                for k in range(PAIRS):
                    r = PAIRS * g + k
                    b = k % 2
                    act.wait_ge(n_transposed, r + 1)
                    if not (first and s == 0 and k < 2):
                        act.wait_ge(n_y, r - 1)
                    nc.scalar.activation(xT[:, b, :], XTb[b][:, :], ACT.Copy).then_inc(n_xT, 1)
                    act.wait_ge(n_y, r + 1)
                    if k == 0 and not (first and s == 0):
                        act.wait_ge(n_squared, PAIRS * 2 * g)
                        act.wait_ge(n_ln, g)
                    for h in range(2):
                        o = h * (H + 1)
                        nc.scalar.activation(junk[:, h, :], YN[k][:, o:o + H], ACT.Square, bias=zero_c[:, :],
                                             accum_out=nss[:, 2 * k + h:2 * k + h + 1]).then_inc(n_squared, 1)
                    gz = YN[k][:, 0:2 * (H + 1)].rearrange("p (h n) -> p h n", h=2)[:, :, H]
                    if k == 0 and not (first and s == 0):
                        act.wait_ge(n_gate, g)
                    nc.scalar.activation(gexp[:, 2 * k:2 * k + 2], gz, ACT.Exp, scale=-1.0, bias=zero_c[:, :]).then_inc(n_small, 1)
                act.wait_ge(n_squared, GT * g + GT)
                nc.scalar.activation(nln[:, :], nss[:, :], ACT.Ln, scale=1.0 / H, bias=eps_c[:, :]).then_inc(n_ln, 1)
                act.wait_ge(n_ln, g + 1)
                if not (first and s == 0):
                    act.wait_ge(n_z, PAIRS * g)
                nc.scalar.activation(nr[:, :], nln[:, :], ACT.Exp, scale=-0.5, bias=zero_c[:, :]).then_inc(n_rstd, 1)
                act.wait_ge(n_mv, g + 1)
                nc.scalar.activation(oln[:, :], mv[:, :, 1], ACT.Ln, scale=1.0, bias=eps_c[:, :]).then_inc(o_ln, 1)
                act.wait_ge(o_ln, g + 1)
                nc.scalar.activation(orr[:, s, :], oln[:, :], ACT.Exp, scale=-0.5, bias=zero_c[:, :]).then_inc(o_r, 1)
                finish(g, s, first)
            groups(act, group)
            act.wait_ge(stored[0], (GROUPS // 2 + 1) * 16)
            act.wait_ge(stored[1], (GROUPS // 2) * 16)

        @block.vector
        def _(dve):
            stats_made = dve.alloc_register("stats_made")
            dve.reg_mov(stats_made, 1)
            done = [0]
            step = setup_step

            def link(ins):
                done[0] += 1
                ins.then_inc(step, 1)
                dve.wait_ge(step, done[0])

            nc.vector.memset(zeros[:, :], 0.0).then_inc(filled, 1)
            link(nc.vector.memset(ones3[:, :], 1.0))
            link(nc.vector.memset(eps_c[:, :], EPS))
            link(nc.vector.memset(zero_c[:, :], 0.0))
            dve.wait_ge(loaded_idx, 64)
            dve.wait_ge(consts, 5)
            link(nc.vector.tensor_copy(key_t[:, :], dst_t[:, :]))
            link(nc.vector.tensor_scalar(above_t[:, :], key_t[:, :], spare_row[:, :], None, ALU.subtract))
            link(nc.vector.tensor_scalar(dgat_t[:, :], key_t[:, :], float(N - 1), None, ALU.min))

            def stage_idx(i, h):
                lo = BODY * i + 4 * h
                nc.vector.tensor_copy(src_i[:, 4 * h:4 * h + 4], src_t[:, bass.ds(lo, 4)])
                nc.vector.tensor_copy(dst_i[:, 4 * h:4 * h + 4], dgat_t[:, bass.ds(lo, 4)]).then_inc(idx_staged, 1)
            stage_idx(0, 0)
            stage_idx(0, 1)

            dve.wait_ge(loaded_w, 16 * 12)
            for j, (raw, cen) in enumerate(((msg_raw, msg_wg), (upd_raw, upd_c))):
                for a in range(2):
                    c = 2 * j + a
                    link(nc.vector.tensor_reduce(neg_mean[:, c:c + 1], raw[:, a, :], AX.X, ALU.add))
                    link(nc.vector.tensor_scalar(neg_mean[:, c:c + 1], neg_mean[:, c:c + 1], -1.0 / H, None, ALU.mult))
                    link(nc.vector.tensor_scalar(cen[:, a, 0:H], raw[:, a, :], neg_mean[:, c:c + 1], None, ALU.add))
            for j, (row, parts) in enumerate(((bias_m, part_m), (bias_u, part_u))):
                c = 4 + j
                link(nc.vector.tensor_reduce(neg_mean[0:1, c:c + 1], bias_raw[:, j, :], AX.X, ALU.add))
                link(nc.vector.tensor_scalar(neg_mean[0:1, c:c + 1], neg_mean[0:1, c:c + 1], -1.0 / H, None, ALU.mult))
                link(nc.vector.tensor_scalar(row[:, 0:H], bias_raw[:, j, :], neg_mean[0:1, c:c + 1], None, ALU.add))
            for a in range(2):
                link(nc.vector.tensor_tensor(msg_wg[:, a, H:2 * H], msg_wg[:, a, 0:H], gains[:, 0, :], ALU.mult))
            link(nc.vector.tensor_tensor(bias_m[:, H:2 * H], bias_m[:, 0:H], gains[0:1, 0, :], ALU.mult))
            made = 0
            for row, parts in ((bias_m, part_m), (bias_u, part_u)):
                for j in range(3):
                    made = made + 1
                    nc.vector.tensor_copy(parts[:, j, :], row[:, :]).then_inc(parts_ready, 1)
                    dve.wait_ge(parts_ready, made)
                    link(nc.vector.tensor_tensor(row[:, :], row[:, :], parts[:, j, :], ALU.subtract))
            nc.vector.memset(upd_c[:, 1, H:H + 1], 0.0).then_inc(setup, 1)

            def body(i, first):
                lo = BODY * i
                if not first:
                    dve.wait_ge(em_made, BODY * i)
                    dve.wait_ge(scat_ready, BODY * i)
                nc.vector.tensor_copy(above_s[:, :], above_t[:, bass.ds(lo, BODY)])
                nc.vector.tensor_copy(w_s[:, :], w_t[:, bass.ds(lo, BODY)])
                nc.vector.tensor_copy(key_s[:, :], key_t[:, bass.ds(lo, BODY)]).then_inc(key_staged, 1)
                dve.wait_ge(key_staged, i + 1)
                for k in range(PAIRS):
                    s = PAIRS * i + k
                    b = k % 2
                    pr = slice(2 * k, 2 * k + 2)
                    dve.wait_ge(transposed, 2 * s + 2)
                    if not (first and k < 2):
                        dve.wait_ge(summed, s - 1)
                    for h in range(2):
                        u = 2 * k + h
                        nc.vector.scalar_tensor_tensor(
                            same[:, 2 * b + h, :], Db[b][:, h * P:(h + 1) * P], key_s[:, u:u + 1], order[:, :],
                            ALU.is_equal, ALU.mult, accum_out=dup[:, u:u + 1]).then_inc(same_made, 1)
                    if k % 2 == 1:
                        stage_idx(i + 1, k // 2)
                    dve.wait_ge(same_made, 2 * s + 2)
                    nc.vector.scalar_tensor_tensor(pick[:, pr], dup[:, pr], 2.0, above_s[:, pr], ALU.is_lt, ALU.mult).then_inc(picked, 1)
                    dve.wait_ge(picked, s + 1)
                    if not first:
                        dve.wait_ge(scattered, 32 * s + 16 * (2 - BODY))
                    nc.vector.tensor_scalar(scat_i[:, pr], pick[:, pr], spare_row[:, :], None, ALU.add).then_inc(scat_ready, 1)
                    nc.vector.tensor_scalar(stage[:, pr, H], dup[:, pr], 1 / LATER, 1 - 1 / LATER, ALU.mult, ALU.add).then_inc(scat_ready, 1)
                    dve.wait_ge(std_ready, s + 1)
                    nc.vector.reciprocal(rstd[:, pr], std[:, pr]).then_inc(rstd_made, 1)
                    dve.wait_ge(rstd_made, s + 1)
                    for h in range(2):
                        u = 2 * k + h
                        nc.vector.scalar_tensor_tensor(
                            z[:, 2 * b + h, :], Yb[b][:, h * 2 * H + H:(h + 1) * 2 * H], rstd[:, u:u + 1], betas[:, 0, :],
                            ALU.mult, ALU.add).then_inc(z_made, 1)
                    for h in range(2):
                        u = 2 * k + h
                        dve.wait_ge(z_made, 2 * s + (h + 1))
                        nc.vector.tensor_scalar(em[:, 2 * b + h, :], z[:, 2 * b + h, :], 0.0, w_s[:, u:u + 1],
                                                ALU.max, ALU.mult).then_inc(em_made, 1)
            bodies(dve, body)

            def scale(g, s, first):
                dve.wait_ge(node_loaded[s], (g // 2 + 1) * 32 if isinstance(g, int) else 16 * g + (32 - 16 * s))
                if not first:
                    dve.wait_ge(mean_made, g - 1)
                nc.vector.tensor_scalar(cnt[:, s, 0, :], tg[:, s, :, H], COUNT_EPS, None, ALU.add).then_inc(cnt_a, 1)
                dve.wait_ge(cnt_a, 2 * g + 1)
                nc.vector.reciprocal(cnt[:, s, 1, :], cnt[:, s, 0, :]).then_inc(cnt_a, 1)
                dve.wait_ge(cnt_a, 2 * g + 2)
                nc.vector.scalar_tensor_tensor(cnt[:, s, 2, :], tg[:, s, :, H], 0.0, cnt[:, s, 1, :],
                                               ALU.is_gt, ALU.mult).then_inc(scale_ready, 1)

            def group(g, s, first):
                nxt = g + 1
                if isinstance(g, int) and nxt == GROUPS:
                    pass
                else:
                    scale(nxt, 1 - s, first and s == 0)
                dve.wait_ge(n_small, PAIRS * g + PAIRS)
                nc.vector.tensor_scalar(gden[:, :], gexp[:, :], 1.0, None, ALU.add).then_inc(n_gate, 1)
                dve.wait_ge(n_gate, g + 1)
                nc.vector.reciprocal(gate[:, :], gden[:, :]).then_inc(n_shift, 1)
                dve.wait_ge(n_shift, 2 * g + 1)
                nc.vector.tensor_scalar(keep[:, :], gate[:, :], -1.0, 2.0, ALU.mult, ALU.add).then_inc(n_shift, 1)
                dve.wait_ge(n_rstd, g + 1)
                for k in range(PAIRS):
                    for h in range(2):
                        t = 2 * k + h
                        last = nc.vector.scalar_tensor_tensor(
                            nbuf[:, t, :], YN[k][:, h * (H + 1):h * (H + 1) + H], nr[:, t:t + 1], gains[:, 1, :],
                            ALU.mult, ALU.mult)
                    last.then_inc(n_z, 1)
                dve.wait_ge(n_z, PAIRS * g + PAIRS)
                nc.vector.tensor_tensor(nbuf[:, :, :], nbuf[:, :, :], betas[:, 1:2, :].broadcast_to([P, GT, H]), ALU.add).then_inc(n_h, 1)
                dve.wait_ge(n_h, 2 * g + 1)
                for t in range(GT):
                    last = nc.vector.tensor_scalar(nbuf[:, t, :], nbuf[:, t, :], 0.0, gate[:, t:t + 1], ALU.max, ALU.mult)
                last.then_inc(n_h, 1)
                dve.wait_ge(n_h, 2 * g + 2)
                dve.wait_ge(n_shift, 2 * g + 2)
                if not first:
                    dve.wait_ge(o_done, g - 1)
                for k in range(PAIRS):
                    for h in range(2):
                        t = 2 * k + h
                        last = nc.vector.scalar_tensor_tensor(
                            yn[:, s, t, :], xg[:, s, t, :], keep[:, t:t + 1], nbuf[:, t, :], ALU.mult, ALU.add)
                    last.then_inc(n_out_y, 1)
                dve.wait_ge(n_out_y, PAIRS * g + PAIRS)
                for t in range(GT):
                    last = nc.vector.bn_stats(stats[:, t, :], yn[:, s, t, :])
                last.then_inc(n_stats, 1)
                if not (first and s == 0):
                    dve.wait_ge(o_ln, g)
                await_next(dve, n_stats, stats_made, 1)
                for t in range(GT):
                    last = nc.vector.bn_aggr(mv[:, t, :], stats[:, t, :])
                last.then_inc(n_mv, 1)
                dve.wait_ge(o_r, g + 1)
                dve.wait_ge(n_mv, g + 1)
                nc.vector.scalar_tensor_tensor(osh[:, s, :], mv[:, :, 0], -1.0, orr[:, s, :], ALU.mult, ALU.mult).then_inc(o_shift, 1)
            scale(0, 0, True)
            groups(dve, group)


_INS = ["x", "src", "dst", "edge_weight", "L0_gnn_msg_w", "L0_gnn_msg_b", "L0_gnn_msg_g", "L0_gnn_msg_beta",
        "L0_gnn_upd_w", "L0_gnn_upd_b", "L0_gnn_upd_g", "L0_gnn_upd_beta", "L0_gnn_gate_w", "L0_gnn_gate_b"]


def kernel(**inputs):
    import numpy as _np
    import concourse.bacc as _bacc
    from concourse import mybir as _mybir
    from concourse.bass_utils import run_bass_kernel_spmd as _run

    nc = _bacc.Bacc("TRN2", target_bir_lowering=False, num_devices=1)
    arrays, args = {}, []
    for name in _INS:
        a = _np.ascontiguousarray(inputs[name])
        arrays[f"in_{name}_dram"] = a
        args.append(nc.dram_tensor(f"in_{name}_dram", a.shape, _mybir.dt.from_np(a.dtype), kind="ExternalInput").ap())
    args.append(nc.dram_tensor("out_0_dram", inputs["x"].shape, _mybir.dt.float32, kind="ExternalOutput").ap())
    build(nc, *args)
    r = _run(nc, [arrays], core_ids=[0])
    return r.results[0]["out_0_dram"]
```

```python
import numpy as np
import concourse.bass as bass
from concourse import mybir
from contextlib import ExitStack

P = 128
F32 = mybir.dt.float32
BF16 = mybir.dt.bfloat16
I32 = mybir.dt.int32
ALU = mybir.AluOpType
ACT = mybir.ActivationFunctionType
AX = mybir.AxisListType
EPS = 1e-5
COUNT_EPS = 1e-8


def build(nc, x, src, dst, edge_w, msg_w, msg_b, msg_g, msg_beta, upd_w, upd_b, upd_g, upd_beta, gate_w, gate_b, out):
    N, H = x.shape
    E = src.shape[0]
    assert H == P
    BODY = 8
    PAIRS = BODY // 2
    BODIES = -(-E // (P * BODY))
    TILES = BODIES * BODY
    FULL = E // TILES
    REST = E - FULL * TILES
    LAG = 7
    ROW = H + 1
    TROWS = P * TILES
    assert TROWS >= N + P and FULL == P - 1
    LATER = 1.0 / 1024
    ZC = 8
    ZROWS = TILES // ZC
    GT = 8
    GN = GT * P
    GROUPS = -(-N // GN)
    GLAST = N - GN
    RING = 4

    table = nc.dram_tensor("table", [TROWS, ROW], F32).ap()

    ctx = ExitStack()
    with ctx:
        def sb(name, shape, dt=F32):
            return ctx.enter_context(nc.sbuf_tensor(name, shape, dt))

        def sem(name):
            return ctx.enter_context(nc.semaphore(name))

        ident = sb("ident", [P, P])
        order = sb("order", [P, P])
        ones3 = sb("ones3", [3, P], BF16)
        zeros = sb("zeros", [P, ZROWS * ROW])
        eps_c = sb("eps_c", [P, 1])
        zero_c = sb("zero_c", [P, 1])
        spare_row = sb("spare_row", [P, 1])
        msg_raw = sb("msg_raw", [P, 2, H])
        msg_wg = sb("msg_wg", [P, 2, 2 * H])
        upd_raw = sb("upd_raw", [P, 2, H])
        upd_c = sb("upd_c", [P, 2, H])
        gate_w_b = sb("gate_w_b", [P, H])
        gate_b_b = sb("gate_b_b", [P, 1])
        neg_mean = sb("neg_mean", [P, 6])
        gains = sb("gains", [P, 2, H])
        betas = sb("betas", [P, 2, H])
        bias_raw = sb("bias_raw", [1, 2, H])
        bias_m = sb("bias_m", [1, 2 * H])
        bias_u = sb("bias_u", [1, H])
        part_m = sb("part_m", [1, 3, 2 * H], BF16)
        part_u = sb("part_u", [1, 3, H], BF16)
        bias3_m = sb("bias3_m", [3, 2 * H], BF16)
        bias3_u = sb("bias3_u", [3, H], BF16)
        src_t = sb("src_t", [P, TILES + BODY], I32)
        dst_t = sb("dst_t", [P, TILES + BODY], I32)
        w_t = sb("w_t", [P, TILES + BODY])
        key_t = sb("key_t", [P, TILES + BODY])
        above_t = sb("above_t", [P, TILES + BODY])
        dgat_t = sb("dgat_t", [P, TILES + BODY])
        src_i = sb("src_i", [P, BODY], I32)
        dst_i = sb("dst_i", [P, BODY], I32)
        key_s = sb("key_s", [P, BODY])
        above_s = sb("above_s", [P, BODY])
        w_s = sb("w_s", [P, BODY])
        rows = sb("rows", [P, BODY, 2, H])
        xT = sb("xT", [P, 2, 4 * P])
        same = sb("same", [P, 4, P])
        dup = sb("dup", [P, BODY])
        pick = sb("pick", [P, BODY])
        scat_i = sb("scat_i", [P, BODY], I32)
        sumsq = sb("sumsq", [P, BODY])
        std = sb("std", [P, BODY])
        rstd = sb("rstd", [P, BODY])
        junk = sb("junk", [P, 2, P])
        z = sb("z", [P, 4, P])
        em = sb("em", [P, 4, P])
        stage = sb("stage", [P, BODY, ROW])
        x_early = sb("x_early", [P, GT, H])
        dot_junk = sb("dot_junk", [P, GT, H])
        dots_s = sb("dots_s", [P, GT])
        dots = sb("dots", [P, GROUPS * GT])
        gates = sb("gates", [P, GROUPS * GT])
        xg = sb("xg", [P, 4, GT, H])
        tg = sb("tg", [P, 2, GT, ROW])
        cnt = sb("cnt", [P, 2, 3, GT])
        mg = sb("mg", [P, 2, GT, H])
        hg = sb("hg", [P, 2, GT, H])
        yg = sb("yg", [P, 2, GT, H])
        og = sb("og", [P, 2, GT, H])
        ss_u = sb("ss_u", [P, GT])
        std_u = sb("std_u", [P, GT])
        rstd_u = sb("rstd_u", [P, 2, GT])
        gate = sb("gate", [P, 2, GT])
        keep = sb("keep", [P, 2, GT])
        stats = sb("stats", [P, GT, 6])
        mv = sb("mv", [P, 2, GT, 2])
        std_o = sb("std_o", [P, GT])
        rstd_o = sb("rstd_o", [P, 2, GT])

        psum = ctx.enter_context(nc.psum_tensor("psum", [P, 8, 512], F32))
        bank = [psum[:, i, :] for i in range(8)]
        XTb, Yb, Db, Ab = bank[0:2], bank[2:4], bank[4:6], bank[6:8]
        YN = bank[2:6]

        loaded_idx = sem("loaded_idx")
        loaded_w = sem("loaded_w")
        filled = sem("filled")
        setup_step = sem("setup_step")
        zeroed = sem("zeroed")
        consts = sem("consts")
        setup = sem("setup")
        parts_ready = sem("parts_ready")
        bias_placed = sem("bias_placed")
        idx_staged = sem("idx_staged")
        key_staged = sem("key_staged")
        gathered = [sem(f"gathered{u}") for u in range(BODY)]
        transposed = sem("transposed")
        xT_ready = sem("xT_ready")
        y_ready = sem("y_ready")
        squared = sem("squared")
        std_ready = sem("std_ready")
        same_made = sem("same_made")
        picked = sem("picked")
        scat_ready = sem("scat_ready")
        rstd_made = sem("rstd_made")
        z_made = sem("z_made")
        em_made = sem("em_made")
        summed = sem("summed")
        staged = sem("staged")
        scattered = sem("scattered")
        x_loaded = [sem(f"x_loaded{i}") for i in range(4)]
        t_loaded = [sem(f"t_loaded{i}") for i in range(2)]
        cnt_step = sem("cnt_step")
        scale_ready = sem("scale_ready")
        mean_made = sem("mean_made")
        n_transposed = sem("n_transposed")
        n_xT = sem("n_xT")
        n_y = sem("n_y")
        n_squared = sem("n_squared")
        n_gate = sem("n_gate")
        n_keep = sem("n_keep")
        n_std = sem("n_std")
        n_rstd = sem("n_rstd")
        n_z = sem("n_z")
        n_beta = sem("n_beta")
        n_h = sem("n_h")
        n_sum = sem("n_sum")
        n_stats = sem("n_stats")
        n_mv = sem("n_mv")
        o_std = sem("o_std")
        o_rstd = sem("o_rstd")
        o_centred = sem("o_centred")
        o_done = sem("o_done")
        early_loaded = sem("early_loaded")
        dots_made = sem("dots_made")
        dotted = sem("dotted")
        gates_made = sem("gates_made")
        stored = [sem(f"stored{i}") for i in range(2)]

        block = ctx.enter_context(nc.Block())

        def await_next(eng, sem, count, due, by):
            if isinstance(count, int):
                eng.wait_ge(sem, count)
            else:
                eng.wait_ge(sem, due)
                eng.reg_add(due, due, by)

        def bodies(eng, body):
            body(0, True)
            with eng.Fori(1, BODIES) as i:
                body(i, False)

        def rounds(eng, turn):
            for j in range(2 * RING):
                turn(j, j % RING)
            with eng.Fori(2, GROUPS // RING - 1) as h:
                for q in range(RING):
                    turn(RING * h + q, q)
            for j in range((GROUPS // RING - 1) * RING, GROUPS + 4):
                turn(j, j % RING)

        def there(g):
            return not isinstance(g, int) or 0 <= g < GROUPS

        def reused(g, ring):
            return not isinstance(g, int) or g >= ring

        def filled_to(g, slot, ring):
            return 16 // ring * (g - slot) + 16

        def base_of(g):
            return GLAST if isinstance(g, int) and g == GROUPS - 1 else g * GN

        @block.sync
        def _(sp):
            sp.wait_ge(filled, 4)
            for t, a in ((src_t, src), (dst_t, dst)):
                sp.dma_start(t[0:FULL, 0:TILES], a[0:FULL * TILES].rearrange("(p t) -> p t", t=TILES)).then_inc(loaded_idx, 16)
                sp.dma_start(t[FULL:P, 0:REST], a[FULL * TILES:E].rearrange("(a t) -> a t", a=1)).then_inc(loaded_idx, 16)
            sp.dma_start(w_t[0:FULL, 0:TILES], edge_w[0:FULL * TILES].rearrange("(p t) -> p t", t=TILES)).then_inc(loaded_w, 16)
            sp.dma_start(w_t[FULL:P, 0:REST], edge_w[FULL * TILES:E].rearrange("(a t) -> a t", a=1)).then_inc(loaded_w, 16)
            sp.dma_start(msg_raw[:, :, :], msg_w.rearrange("(a p) n -> p a n", p=P)).then_inc(loaded_w, 16)
            sp.dma_start(upd_raw[:, :, :], upd_w.rearrange("(a p) n -> p a n", p=P)).then_inc(loaded_w, 16)
            sp.dma_start(gate_w_b[:, :], gate_w.rearrange("n a -> a n").broadcast_to([P, H])).then_inc(loaded_w, 16)
            for j, (g, b) in enumerate(((msg_g, msg_beta), (upd_g, upd_beta))):
                sp.dma_start(gains[:, j, :], g.rearrange("(a n) -> a n", a=1).broadcast_to([P, H])).then_inc(loaded_w, 16)
                sp.dma_start(betas[:, j, :], b.rearrange("(a n) -> a n", a=1).broadcast_to([P, H])).then_inc(loaded_w, 16)
            sp.dma_start(bias_raw[:, 0, :], msg_b.rearrange("(a n) -> a n", a=1)).then_inc(loaded_w, 16)
            sp.dma_start(bias_raw[:, 1, :], upd_b.rearrange("(a n) -> a n", a=1)).then_inc(loaded_w, 16)
            sp.dma_start(gate_b_b[:, :], gate_b.rearrange("(a n) -> a n", a=1).broadcast_to([P, 1])).then_inc(loaded_w, 16)
            zview = table.rearrange("(p c r) n -> p c (r n)", c=ZC, r=ZROWS)
            for c in range(ZC):
                sp.dma_start(zview[:, c, :], zeros[:, :]).then_inc(zeroed, 16)
            sp.wait_ge(parts_ready, 6)
            for j in range(3):
                sp.dma_start(bias3_m[j:j + 1, :], part_m[:, j, :]).then_inc(bias_placed, 16)
                sp.dma_start(bias3_u[j:j + 1, :], part_u[:, j, :]).then_inc(bias_placed, 16)

            def load_early(g):
                if reused(g, 1):
                    sp.wait_ge(dotted, g)
                sp.dma_start(x_early[:, :, :].rearrange("p t n -> p (t n)"),
                             x[bass.ds(base_of(g), GN), :].rearrange("(p t) n -> p (t n)", t=GT)).then_inc(early_loaded, 16)
            load_early(0)
            with sp.Fori(1, GROUPS - 1) as g:
                load_early(g)
            load_early(GROUPS - 1)

            def load_x(g, s):
                if reused(g, 4):
                    sp.wait_ge(n_sum, g - 3)
                sp.dma_start(xg[:, s, :, :].rearrange("p t n -> p (t n)"),
                             x[bass.ds(base_of(g), GN), :].rearrange("(p t) n -> p (t n)", t=GT)).then_inc(x_loaded[s], 16)

            def load_t(g, s):
                if reused(g, 2):
                    sp.wait_ge(mean_made, g - 1)
                sp.dma_start(tg[:, s, :, :].rearrange("p t n -> p (t n)"),
                             table[bass.ds(base_of(g), GN), :].rearrange("(p t) n -> p (t n)", t=GT)).then_inc(t_loaded[s], 16)

            def store(g, s):
                sp.wait_ge(o_done, g + 1)
                if isinstance(g, int) and g == GROUPS - 1:
                    sp.wait_ge(stored[1 - s], filled_to(g - 1, 1 - s, 2))
                sp.dma_start(out[bass.ds(base_of(g), GN), :].rearrange("(p t) n -> p (t n)", t=GT),
                             og[:, s, :, :].rearrange("p t n -> p (t n)")).then_inc(stored[s], 16)

            load_x(0, 0)
            sp.wait_ge(scattered, 16 * TILES)
            load_t(0, 0)
            load_t(1, 1)

            def turn(j, q):
                if there(j + 2):
                    load_t(j + 2, q % 2)
                if there(j + 1):
                    load_x(j + 1, (q + 1) % 4)
                if there(j - 4):
                    store(j - 4, q % 2)
            rounds(sp, turn)
            for s in range(2):
                last = GROUPS - 1 if (GROUPS - 1) % 2 == s else GROUPS - 2
                sp.wait_ge(stored[s], filled_to(last, s, 2))

        @block.gpsimd
        def _(pool):
            slot_used = pool.alloc_register("slot_used")
            before = pool.alloc_register("before")
            pool.reg_mov(slot_used, 1)
            pool.reg_mov(before, 16 * (BODY - LAG))
            nc.gpsimd.memset(src_t[:, :], 0).then_inc(filled, 1)
            nc.gpsimd.memset(dst_t[:, :], N + P - 1).then_inc(filled, 1)
            nc.gpsimd.memset(w_t[:, :], 0.0).then_inc(filled, 1)
            nc.gpsimd.memset(ident[:, :], 0.0).then_inc(consts, 1)
            nc.gpsimd.memset(order[:, :], 1.0).then_inc(consts, 1)
            pool.wait_ge(consts, 2)
            nc.gpsimd.affine_select(out=ident[:, :], in_=ident[:, :], compare_op=ALU.not_equal, fill=1.0,
                                    base=0, pattern=[[-1, P]], channel_multiplier=1).then_inc(consts, 1)
            nc.gpsimd.affine_select(out=order[:, :], in_=order[:, :], compare_op=ALU.is_ge, fill=LATER,
                                    base=0, pattern=[[1, P]], channel_multiplier=-1).then_inc(consts, 1)
            nc.gpsimd.iota(spare_row[:, :], pattern=[[0, 1]], base=N, channel_multiplier=1,
                           allow_small_or_imprecise_dtypes=True).then_inc(consts, 1)

            def gather(t, u, first):
                if u % 4 == 0:
                    pool.wait_ge(idx_staged, 2 * t + u // 4 + 1)
                if not first:
                    await_next(pool, transposed, BODY * t + (u - BODY + 1), slot_used, 1)
                for j, idx in ((0, src_i), (1, dst_i)):
                    nc.gpsimd.indirect_dma_start(
                        rows[:, u, j, :], None, x, bass.IndirectOffsetOnAxis(ap=idx[:, u:u + 1], axis=0)
                    ).then_inc(gathered[u], 16)

            def scatter(i, u):
                pool.wait_ge(staged, PAIRS * i + (u // 2 + 1))
                pool.wait_ge(scat_ready, 2 * (PAIRS * i + (u // 2 + 1)))
                if isinstance(i, int) and i == 0 and u == 0:
                    pool.wait_ge(zeroed, 16 * ZC)
                else:
                    await_next(pool, scattered, 16 * (BODY * i + u), before, 16)
                nc.gpsimd.indirect_dma_start(
                    table, bass.IndirectOffsetOnAxis(ap=scat_i[:, u:u + 1], axis=0), stage[:, u, :], None,
                    compute_op=ALU.add).then_inc(scattered, 16)

            def body(i, first):
                for u in range(BODY):
                    if u >= LAG:
                        scatter(i, u - LAG)
                    elif not first:
                        scatter(i - 1, u - LAG + BODY)
                    gather(i, u, first)
            bodies(pool, body)
            for u in range(BODY - LAG, BODY):
                scatter(BODIES - 1, u)

            def mean(g, s):
                pool.wait_ge(scale_ready, g + 1)
                if reused(g, 2):
                    pool.wait_ge(n_transposed, PAIRS * (g - 1))
                nc.gpsimd.tensor_tensor(mg[:, s, :, :], tg[:, s, :, 0:H],
                                        cnt[:, s, 2, :].unsqueeze(2).broadcast_to([P, GT, H]), ALU.mult).then_inc(mean_made, 1)

            def add_beta(g, s):
                pool.wait_ge(n_z, PAIRS * g + PAIRS)
                nc.gpsimd.tensor_tensor(hg[:, s, :, :], hg[:, s, :, :], betas[:, 1:2, :].broadcast_to([P, GT, H]),
                                        ALU.add).then_inc(n_beta, 1)

            def norm_out(g, s):
                pool.wait_ge(n_mv, g + 1)
                if reused(g, 2):
                    pool.wait_ge(stored[s], filled_to(g - 2, s, 2))
                nc.gpsimd.tensor_tensor(og[:, s, :, :], yg[:, s, :, :],
                                        mv[:, s, :, 0:1].broadcast_to([P, GT, H]), ALU.subtract).then_inc(o_centred, 1)
                pool.wait_ge(o_rstd, g + 1)
                pool.wait_ge(o_centred, g + 1)
                nc.gpsimd.tensor_tensor(og[:, s, :, :], og[:, s, :, :],
                                        rstd_o[:, s, :].unsqueeze(2).broadcast_to([P, GT, H]), ALU.mult).then_inc(o_done, 1)

            mean(0, 0)

            def turn(j, q):
                if there(j - 1):
                    add_beta(j - 1, (q - 1) % 2)
                if there(j + 1):
                    mean(j + 1, (q + 1) % 2)
                if there(j - 3):
                    norm_out(j - 3, (q - 3) % 2)
            rounds(pool, turn)

        @block.tensor
        def _(pe):
            pe.wait_ge(consts, 5)
            pe.wait_ge(bias_placed, 96)
            pe.wait_ge(setup, 1)

            def transposes(i, k):
                s = PAIRS * i + k
                b = k % 2
                if k == 0:
                    pe.wait_ge(key_staged, i + 1)
                for h in range(2):
                    u = 2 * k + h
                    nc.tensor.transpose(Db[b][:, h * P:(h + 1) * P], key_s[:, u:u + 1].broadcast_to([P, P]), ident[:, :])
                for h in range(2):
                    u = 2 * k + h
                    pe.wait_ge(gathered[u], 32 * i + 32)
                    for j in range(2):
                        last = nc.tensor.transpose(XTb[b][:, (2 * h + j) * P:(2 * h + j + 1) * P], rows[:, u, j, :], ident[:, :])
                    last.then_inc(transposed, 1)

            def products(i, k):
                b = k % 2
                pe.wait_ge(xT_ready, PAIRS * i + (k + 1))
                for h in range(2):
                    o = Yb[b][:, h * 2 * H:(h + 1) * 2 * H]
                    nc.tensor.matmul(o, ones3[:, :], bias3_m[:, :], start=True, stop=False)
                    nc.tensor.matmul(o, xT[:, b, 2 * h * P:(2 * h + 1) * P], msg_wg[:, 0, :], start=False, stop=False)
                    last = nc.tensor.matmul(o, xT[:, b, (2 * h + 1) * P:(2 * h + 2) * P], msg_wg[:, 1, :], start=False, stop=True)
                last.then_inc(y_ready, 1)

            def sums(s, b, early):
                pe.wait_ge(em_made, 2 * s + 2)
                if not early:
                    pe.wait_ge(staged, s - 1)
                for h in range(2):
                    q = 2 * b + h
                    last = nc.tensor.matmul(Ab[b][:, h * P:(h + 1) * P], same[:, q, :], em[:, q, :], start=True, stop=True)
                last.then_inc(summed, 1)

            def body(i, first):
                for k in range(PAIRS):
                    transposes(i, k)
                    if not (first and k == 0):
                        sums(PAIRS * i + (k - 1), (k - 1) % 2, first and k <= 2)
                    products(i, k)
            bodies(pe, body)
            sums(PAIRS * BODIES - 1, 1, False)

            pe.wait_ge(staged, PAIRS * BODIES)

            def turn(g, q):
                if not there(g):
                    return

                def node_transposes(k):
                    b = k % 2
                    if reused(g, 1) or k >= 2:
                        pe.wait_ge(n_xT, PAIRS * g + (k - 1))
                    for h in range(2):
                        t = 2 * k + h
                        nc.tensor.transpose(XTb[b][:, 2 * h * P:(2 * h + 1) * P], xg[:, q, t, :], ident[:, :])
                        last = nc.tensor.transpose(XTb[b][:, (2 * h + 1) * P:(2 * h + 2) * P], mg[:, q % 2, t, :], ident[:, :])
                    last.then_inc(n_transposed, 1)

                pe.wait_ge(x_loaded[q], filled_to(g, q, 4))
                pe.wait_ge(mean_made, g + 1)
                node_transposes(0)
                for k in range(PAIRS):
                    r = PAIRS * g + k
                    b = k % 2
                    if k + 1 < PAIRS:
                        node_transposes(k + 1)
                    pe.wait_ge(n_xT, r + 1)
                    if reused(g, 1):
                        pe.wait_ge(n_z, r - (PAIRS - 1))
                    for h in range(2):
                        o = YN[k][:, h * H:(h + 1) * H]
                        nc.tensor.matmul(o, ones3[:, :], bias3_u[:, :], start=True, stop=False)
                        nc.tensor.matmul(o, xT[:, b, 2 * h * P:(2 * h + 1) * P], upd_c[:, 0, :], start=False, stop=False)
                        last = nc.tensor.matmul(o, xT[:, b, (2 * h + 1) * P:(2 * h + 2) * P], upd_c[:, 1, :], start=False, stop=True)
                    last.then_inc(n_y, 1)
            rounds(pe, turn)

        @block.scalar
        def _(act):
            act.wait_ge(setup, 1)

            def evacuate(i, k, first):
                s = PAIRS * i + k
                b = k % 2
                act.wait_ge(transposed, 2 * s + 2)
                if not (first and k < 2):
                    act.wait_ge(y_ready, s - 1)
                nc.scalar.activation(xT[:, b, :], XTb[b][:, :], ACT.Copy).then_inc(xT_ready, 1)

            def variances(i, k, first):
                s = PAIRS * i + k
                b = k % 2
                act.wait_ge(y_ready, s + 1)
                if not (first and k == 0):
                    act.wait_ge(squared, 2 * s)
                for h in range(2):
                    u = 2 * k + h
                    nc.scalar.activation(junk[:, h, :], Yb[b][:, h * 2 * H:h * 2 * H + H], ACT.Square,
                                         accum_out=sumsq[:, u:u + 1]).then_inc(squared, 1)
                act.wait_ge(squared, 2 * s + 2)
                nc.scalar.activation(std[:, 2 * k:2 * k + 2], sumsq[:, 2 * k:2 * k + 2], ACT.Sqrt, bias=eps_c[:, :],
                                     scale=1.0 / H).then_inc(std_ready, 1)

            def sums(s, k, no_scatter):
                b = k % 2
                act.wait_ge(summed, s + 1)
                if not no_scatter:
                    act.wait_ge(scattered, 32 * s + 16 * (2 - BODY))
                nc.scalar.activation(stage[:, 2 * k:2 * k + 2, 0:H], Ab[b][:, 0:2 * P].rearrange("p (h n) -> p h n", h=2),
                                     ACT.Copy).then_inc(staged, 1)

            def body(i, first):
                for k in range(PAIRS):
                    evacuate(i, k, first)
                    if not (first and k == 0):
                        sums(PAIRS * i + (k - 1), (k - 1) % PAIRS, first)
                    variances(i, k, first)
            body(0, True)
            with act.Fori(1, BODIES) as i:
                body(i, False)
            sums(PAIRS * BODIES - 1, PAIRS - 1, False)
            act.wait_ge(dotted, GROUPS)
            nc.scalar.activation(gates[:, :], dots[:, :], ACT.Sigmoid, bias=gate_b_b[:, :]).then_inc(gates_made, 1)

            def front(g, s):
                for k in range(PAIRS):
                    r = PAIRS * g + k
                    b = k % 2
                    act.wait_ge(n_transposed, r + 1)
                    if reused(g, 1) or k >= 2:
                        act.wait_ge(n_y, r - 1)
                    nc.scalar.activation(xT[:, b, :], XTb[b][:, :], ACT.Copy).then_inc(n_xT, 1)
                    act.wait_ge(n_y, r + 1)
                    if k == 0 and reused(g, 1):
                        act.wait_ge(n_squared, GT * g)
                        act.wait_ge(n_std, g)
                    for h in range(2):
                        nc.scalar.activation(junk[:, h, :], YN[k][:, h * H:(h + 1) * H], ACT.Square,
                                             accum_out=ss_u[:, 2 * k + h:2 * k + h + 1]).then_inc(n_squared, 1)
                act.wait_ge(n_squared, GT * g + GT)
                if reused(g, 1):
                    act.wait_ge(n_rstd, g)
                nc.scalar.activation(std_u[:, :], ss_u[:, :], ACT.Sqrt, scale=1.0 / H, bias=eps_c[:, :]).then_inc(n_std, 1)

            def std_out(g, s):
                act.wait_ge(n_mv, g + 1)
                if reused(g, 1):
                    act.wait_ge(o_rstd, g)
                nc.scalar.activation(std_o[:, :], mv[:, s, :, 1], ACT.Sqrt, bias=eps_c[:, :]).then_inc(o_std, 1)

            def gated(g, s):
                act.wait_ge(n_beta, g + 1)
                act.wait_ge(n_gate, g + 1)
                for t in range(GT):
                    last = nc.scalar.activation(hg[:, s, t, :], hg[:, s, t, :], ACT.Relu,
                                                scale=gate[:, s, t:t + 1])
                last.then_inc(n_h, 1)

            def turn(j, q):
                if there(j):
                    front(j, q % 2)
                if there(j - 1):
                    gated(j - 1, (q - 1) % 2)
                if there(j - 2):
                    std_out(j - 2, (q - 2) % 2)
            rounds(act, turn)

        @block.vector
        def _(dve):
            stats_made = dve.alloc_register("stats_made")
            dve.reg_mov(stats_made, 2 * RING - 1)
            done = [0]
            step = setup_step

            def link(ins):
                done[0] += 1
                ins.then_inc(step, 1)
                dve.wait_ge(step, done[0])

            nc.vector.memset(zeros[:, :], 0.0).then_inc(filled, 1)
            link(nc.vector.memset(ones3[:, :], 1.0))
            link(nc.vector.memset(eps_c[:, :], EPS))
            dve.wait_ge(loaded_idx, 64)
            dve.wait_ge(consts, 5)
            link(nc.vector.tensor_copy(key_t[:, :], dst_t[:, :]))
            link(nc.vector.tensor_scalar(above_t[:, :], key_t[:, :], spare_row[:, :], None, ALU.subtract))
            link(nc.vector.tensor_scalar(dgat_t[:, :], key_t[:, :], float(N - 1), None, ALU.min))

            def stage_idx(i, h):
                lo = BODY * i + 4 * h
                nc.vector.tensor_copy(src_i[:, 4 * h:4 * h + 4], src_t[:, bass.ds(lo, 4)])
                nc.vector.tensor_copy(dst_i[:, 4 * h:4 * h + 4], dgat_t[:, bass.ds(lo, 4)]).then_inc(idx_staged, 1)
            stage_idx(0, 0)
            stage_idx(0, 1)

            dve.wait_ge(loaded_w, 16 * 12)
            for j, (raw, cen) in enumerate(((msg_raw, msg_wg), (upd_raw, upd_c))):
                for a in range(2):
                    c = 2 * j + a
                    link(nc.vector.tensor_reduce(neg_mean[:, c:c + 1], raw[:, a, :], AX.X, ALU.add))
                    link(nc.vector.tensor_scalar(neg_mean[:, c:c + 1], neg_mean[:, c:c + 1], -1.0 / H, None, ALU.mult))
                    link(nc.vector.tensor_scalar(cen[:, a, 0:H], raw[:, a, :], neg_mean[:, c:c + 1], None, ALU.add))
            for j, (row, parts) in enumerate(((bias_m, part_m), (bias_u, part_u))):
                c = 4 + j
                link(nc.vector.tensor_reduce(neg_mean[0:1, c:c + 1], bias_raw[:, j, :], AX.X, ALU.add))
                link(nc.vector.tensor_scalar(neg_mean[0:1, c:c + 1], neg_mean[0:1, c:c + 1], -1.0 / H, None, ALU.mult))
                link(nc.vector.tensor_scalar(row[:, 0:H], bias_raw[:, j, :], neg_mean[0:1, c:c + 1], None, ALU.add))
            for a in range(2):
                link(nc.vector.tensor_tensor(msg_wg[:, a, H:2 * H], msg_wg[:, a, 0:H], gains[:, 0, :], ALU.mult))
            link(nc.vector.tensor_tensor(bias_m[:, H:2 * H], bias_m[:, 0:H], gains[0:1, 0, :], ALU.mult))
            made = 0
            for row, parts in ((bias_m, part_m), (bias_u, part_u)):
                for j in range(3):
                    made = made + 1
                    nc.vector.tensor_copy(parts[:, j, :], row[:, :]).then_inc(parts_ready, 1)
                    dve.wait_ge(parts_ready, made)
                    link(nc.vector.tensor_tensor(row[:, :], row[:, :], parts[:, j, :], ALU.subtract))
            nc.vector.memset(zero_c[:, :], 0.0).then_inc(setup, 1)

            def body(i, first):
                lo = BODY * i
                if not first:
                    dve.wait_ge(em_made, BODY * i)
                    dve.wait_ge(scat_ready, BODY * i)
                nc.vector.tensor_copy(above_s[:, :], above_t[:, bass.ds(lo, BODY)])
                nc.vector.tensor_copy(w_s[:, :], w_t[:, bass.ds(lo, BODY)])
                nc.vector.tensor_copy(key_s[:, :], key_t[:, bass.ds(lo, BODY)]).then_inc(key_staged, 1)
                dve.wait_ge(key_staged, i + 1)
                for k in range(PAIRS):
                    s = PAIRS * i + k
                    b = k % 2
                    pr = slice(2 * k, 2 * k + 2)
                    dve.wait_ge(transposed, 2 * s + 2)
                    if not (first and k < 2):
                        dve.wait_ge(summed, s - 1)
                    for h in range(2):
                        u = 2 * k + h
                        nc.vector.scalar_tensor_tensor(
                            same[:, 2 * b + h, :], Db[b][:, h * P:(h + 1) * P], key_s[:, u:u + 1], order[:, :],
                            ALU.is_equal, ALU.mult, accum_out=dup[:, u:u + 1]).then_inc(same_made, 1)
                    if k % 2 == 1:
                        stage_idx(i + 1, k // 2)
                    dve.wait_ge(same_made, 2 * s + 2)
                    nc.vector.scalar_tensor_tensor(pick[:, pr], dup[:, pr], 2.0, above_s[:, pr], ALU.is_lt, ALU.mult).then_inc(picked, 1)
                    dve.wait_ge(picked, s + 1)
                    if not first:
                        dve.wait_ge(scattered, 32 * s + 16 * (2 - BODY))
                    nc.vector.tensor_scalar(scat_i[:, pr], pick[:, pr], spare_row[:, :], None, ALU.add).then_inc(scat_ready, 1)
                    nc.vector.tensor_scalar(stage[:, pr, H], dup[:, pr], 1 / LATER, 1 - 1 / LATER, ALU.mult, ALU.add).then_inc(scat_ready, 1)
                    dve.wait_ge(std_ready, s + 1)
                    nc.vector.reciprocal(rstd[:, pr], std[:, pr]).then_inc(rstd_made, 1)
                    dve.wait_ge(rstd_made, s + 1)
                    for h in range(2):
                        u = 2 * k + h
                        nc.vector.scalar_tensor_tensor(
                            z[:, 2 * b + h, :], Yb[b][:, h * 2 * H + H:(h + 1) * 2 * H], rstd[:, u:u + 1], betas[:, 0, :],
                            ALU.mult, ALU.add).then_inc(z_made, 1)
                    for h in range(2):
                        u = 2 * k + h
                        dve.wait_ge(z_made, 2 * s + (h + 1))
                        nc.vector.tensor_scalar(em[:, 2 * b + h, :], z[:, 2 * b + h, :], 0.0, w_s[:, u:u + 1],
                                                ALU.max, ALU.mult).then_inc(em_made, 1)
                    if k == 0:
                        dve.wait_ge(early_loaded, 16 * i + 16)
                        if not first:
                            dve.wait_ge(dotted, i)
                    for t in (2 * k, 2 * k + 1):
                        nc.vector.scalar_tensor_tensor(dot_junk[:, t, :], x_early[:, t, :], 1.0, gate_w_b[:, :], ALU.mult, ALU.mult,
                                                       accum_out=dots_s[:, t:t + 1]).then_inc(dots_made, 1)
                dve.wait_ge(dots_made, GT * i + GT)
                nc.vector.tensor_copy(dots[:, bass.ds(GT * i, GT)], dots_s[:, :]).then_inc(dotted, 1)
            bodies(dve, body)

            def scale(g, s):
                dve.wait_ge(t_loaded[s], filled_to(g, s, 2))
                if reused(g, 2):
                    dve.wait_ge(mean_made, g - 1)
                nc.vector.tensor_scalar(cnt[:, s, 0, :], tg[:, s, :, H], COUNT_EPS, None, ALU.add).then_inc(cnt_step, 1)
                dve.wait_ge(cnt_step, 2 * g + 1)
                nc.vector.reciprocal(cnt[:, s, 1, :], cnt[:, s, 0, :]).then_inc(cnt_step, 1)
                dve.wait_ge(cnt_step, 2 * g + 2)
                nc.vector.scalar_tensor_tensor(cnt[:, s, 2, :], tg[:, s, :, H], 0.0, cnt[:, s, 1, :],
                                               ALU.is_gt, ALU.mult).then_inc(scale_ready, 1)

            def norm_update(g, s):
                if reused(g, 2):
                    dve.wait_ge(n_sum, g - 1)
                these = gates[:, bass.ds(GT * g, GT)]
                nc.vector.tensor_copy(gate[:, s, :], these).then_inc(n_gate, 1)
                nc.vector.tensor_scalar(keep[:, s, :], these, -1.0, 2.0, ALU.mult, ALU.add).then_inc(n_keep, 1)
                dve.wait_ge(n_std, g + 1)
                if reused(g, 2):
                    dve.wait_ge(n_z, PAIRS * (g - 1))
                nc.vector.reciprocal(rstd_u[:, s, :], std_u[:, :]).then_inc(n_rstd, 1)
                dve.wait_ge(n_rstd, g + 1)
                for k in range(PAIRS):
                    for h in range(2):
                        t = 2 * k + h
                        last = nc.vector.scalar_tensor_tensor(
                            hg[:, s, t, :], YN[k][:, h * H:(h + 1) * H], rstd_u[:, s, t:t + 1], gains[:, 1, :],
                            ALU.mult, ALU.mult)
                    last.then_inc(n_z, 1)

            def residual(g, s, xs):
                dve.wait_ge(n_h, g + 1)
                dve.wait_ge(n_keep, g + 1)
                if reused(g, 2):
                    dve.wait_ge(o_centred, g - 1)
                    dve.wait_ge(n_mv, g)
                for t in range(GT):
                    last = nc.vector.scalar_tensor_tensor(
                        yg[:, s, t, :], xg[:, xs, t, :], keep[:, s, t:t + 1], hg[:, s, t, :], ALU.mult, ALU.add)
                last.then_inc(n_sum, 1)
                dve.wait_ge(n_sum, g + 1)
                for t in range(GT):
                    last = nc.vector.bn_stats(stats[:, t, :], yg[:, s, t, :])
                last.then_inc(n_stats, 1)
                if reused(g, 2):
                    dve.wait_ge(o_std, g - 1)
                await_next(dve, n_stats, g + 1, stats_made, 1)
                for t in range(GT):
                    last = nc.vector.bn_aggr(mv[:, s, t, :], stats[:, t, :])
                last.then_inc(n_mv, 1)

            def rstd_out(g, s):
                dve.wait_ge(o_std, g + 1)
                if reused(g, 2):
                    dve.wait_ge(o_done, g - 1)
                nc.vector.reciprocal(rstd_o[:, s, :], std_o[:, :]).then_inc(o_rstd, 1)

            scale(0, 0)
            dve.wait_ge(gates_made, 1)

            def turn(j, q):
                if there(j - 1):
                    norm_update(j - 1, (q - 1) % 2)
                if there(j - 3):
                    rstd_out(j - 3, (q - 3) % 2)
                if there(j - 2):
                    residual(j - 2, (q - 2) % 2, (q - 2) % 4)
                if there(j + 1):
                    scale(j + 1, (q + 1) % 2)
            rounds(dve, turn)


_INS = ["x", "src", "dst", "edge_weight", "L0_gnn_msg_w", "L0_gnn_msg_b", "L0_gnn_msg_g", "L0_gnn_msg_beta",
        "L0_gnn_upd_w", "L0_gnn_upd_b", "L0_gnn_upd_g", "L0_gnn_upd_beta", "L0_gnn_gate_w", "L0_gnn_gate_b"]


def kernel(**inputs):
    import numpy as _np
    import concourse.bacc as _bacc
    from concourse import mybir as _mybir
    from concourse.bass_utils import run_bass_kernel_spmd as _run

    nc = _bacc.Bacc("TRN2", target_bir_lowering=False, num_devices=1)
    arrays, args = {}, []
    for name in _INS:
        a = _np.ascontiguousarray(inputs[name])
        arrays[f"in_{name}_dram"] = a
        args.append(nc.dram_tensor(f"in_{name}_dram", a.shape, _mybir.dt.from_np(a.dtype), kind="ExternalInput").ap())
    args.append(nc.dram_tensor("out_0_dram", inputs["x"].shape, _mybir.dt.float32, kind="ExternalOutput").ap())
    build(nc, *args)
    r = _run(nc, [arrays], core_ids=[0])
    return r.results[0]["out_0_dram"]
```

```python
import numpy as np
import concourse.bass as bass
from concourse import mybir
from contextlib import ExitStack

P = 128
F32 = mybir.dt.float32
BF16 = mybir.dt.bfloat16
I32 = mybir.dt.int32
ALU = mybir.AluOpType
ACT = mybir.ActivationFunctionType
AX = mybir.AxisListType
EPS = 1e-5
COUNT_EPS = 1e-8


def build(nc, x, src, dst, edge_w, msg_w, msg_b, msg_g, msg_beta, upd_w, upd_b, upd_g, upd_beta, gate_w, gate_b, out):
    N, H = x.shape
    E = src.shape[0]
    assert H == P
    BODY = 8
    PAIRS = BODY // 2
    BODIES = -(-E // (P * BODY))
    TILES = BODIES * BODY
    BE = P * BODY
    REST = E - (BODIES - 1) * BE
    LAG = 7
    ROW = H + 1
    SPACE = P * TILES
    TROWS = SPACE + BE
    assert SPACE >= N + P and 0 < REST <= BE and BE == 1024
    LATER = 1.0 / 1024
    ZC = 40
    ZROWS = TROWS // (P * ZC)
    assert ZROWS * P * ZC == TROWS
    ZFIRST = 8
    ZBODIES = 3
    ZSTART = (ZC - ZFIRST) * ZROWS * P
    GT = 8
    GN = GT * P
    GROUPS = -(-N // GN)
    assert GROUPS == BODIES
    UT = 2
    UNITS = PAIRS * GROUPS
    DELAY = 2 * PAIRS
    PEELED = 5
    XRING = 8
    PAUSE = 6
    DEPTH = 9

    table = nc.dram_tensor("table", [TROWS, ROW], F32).ap()

    ctx = ExitStack()
    with ctx:
        def sb(name, shape, dt=F32):
            return ctx.enter_context(nc.sbuf_tensor(name, shape, dt))

        def sem(name):
            return ctx.enter_context(nc.semaphore(name))

        ident = sb("ident", [P, P])
        order = sb("order", [P, P])
        ones3 = sb("ones3", [3, P], BF16)
        zeros = sb("zeros", [P, ZROWS * ROW])
        eps_c = sb("eps_c", [P, 1])
        zero_c = sb("zero_c", [P, 1])
        spare_row = sb("spare_row", [P, 1])
        msg_raw = sb("msg_raw", [P, 2, H])
        msg_wg = sb("msg_wg", [P, 2, 2 * H])
        upd_raw = sb("upd_raw", [P, 2, H])
        upd_wg = sb("upd_wg", [P, 2, 2 * H])
        reverse = sb("reverse", [BODIES, BODIES])
        gate_w_b = sb("gate_w_b", [P, H])
        gate_b_b = sb("gate_b_b", [P, 1])
        neg_mean = sb("neg_mean", [P, 6])
        gains = sb("gains", [P, 2, H])
        betas = sb("betas", [P, 2, H])
        ones_c = sb("ones_c", [P, 1])
        bias_raw = sb("bias_raw", [1, 2, H])
        bias_m = sb("bias_m", [1, 2 * H])
        bias_u = sb("bias_u", [1, 2 * H])
        part_m = sb("part_m", [1, 3, 2 * H], BF16)
        part_u = sb("part_u", [1, 3, 2 * H], BF16)
        bias3_m = sb("bias3_m", [3, 2 * H], BF16)
        bias3_u = sb("bias3_u", [3, 2 * H], BF16)
        src_raw = sb("src_raw", [BODIES, BE], I32)
        dst_raw = sb("dst_raw", [BODIES, BE], I32)
        raw3 = sb("raw3", [BODIES, 3, BE])
        bound_t = sb("bound_t", [P, TILES])
        worst = sb("worst", [P, 4])
        redo_f = sb("redo_f", [1, 2])
        redo = sb("redo", [1, 6], I32)
        src_t = sb("src_t", [P, TILES + BODY], I32)
        w_t = sb("w_t", [P, TILES + BODY])
        key_t = sb("key_t", [P, TILES + BODY])
        above_t = sb("above_t", [P, TILES + BODY])
        dgat_t = sb("dgat_t", [P, TILES + BODY])
        src_i = sb("src_i", [P, BODY], I32)
        dst_i = sb("dst_i", [P, BODY], I32)
        key_s = sb("key_s", [P, 2, BODY])
        above_s = sb("above_s", [P, 2, BODY])
        w_s = sb("w_s", [P, 2, BODY])
        rows = sb("rows", [P, BODY, 2, H])
        xT = sb("xT", [P, 2, 4 * P])
        same = sb("same", [P, 4, P])
        dup = sb("dup", [P, BODY])
        pick = sb("pick", [P, BODY])
        scat_i = sb("scat_i", [P, BODY], I32)
        sumsq = sb("sumsq", [P, BODY])
        std = sb("std", [P, BODY])
        rstd = sb("rstd", [P, BODY])
        junk = sb("junk", [P, 2, P])
        z = sb("z", [P, 4, P])
        em = sb("em", [P, 4, P])
        stage = sb("stage", [P, BODY, ROW])
        x_early = sb("x_early", [P, XRING, UT, H])
        dot_junk = sb("dot_junk", [P, GT, H])
        dots = sb("dots", [P, 2, GT])
        gates = sb("gates", [P, GROUPS * GT])
        xg = sb("xg", [P, XRING, UT, H])
        tg = sb("tg", [P, XRING, UT, ROW])
        cnt = sb("cnt", [P, 4, 3, UT])
        mg = sb("mg", [P, 4, UT, H])
        nT = sb("nT", [P, 2, 2 * UT, P])
        hg = sb("hg", [P, 4, UT, H])
        yg = sb("yg", [P, 4, UT, H])
        og = sb("og", [P, 4, UT, H])
        nsq = sb("nsq", [P, UT, H])
        ss_u = sb("ss_u", [P, 4, UT])
        std_u = sb("std_u", [P, 4, UT])
        rstd_u = sb("rstd_u", [P, 4, UT])
        gate = sb("gate", [P, 2, GT])
        keep = sb("keep", [P, 2, GT])
        stats = sb("stats", [P, 2, UT, 6])
        mv = sb("mv", [P, 4, UT, 2])
        std_o = sb("std_o", [P, 4, UT])
        rstd_o = sb("rstd_o", [P, 4, UT])

        psum = ctx.enter_context(nc.psum_tensor("psum", [P, 8, 512], F32))
        bank = [psum[:, i, :] for i in range(8)]
        XTb, Yb, Db, Ab = bank[0:4]
        XTn, Yn = bank[4:6], bank[6:8]

        loaded_idx = sem("loaded_idx")
        loaded_w = sem("loaded_w")
        filled = sem("filled")
        setup_step = sem("setup_step")
        consts = sem("consts")
        setup = sem("setup")
        parts_ready = sem("parts_ready")
        bias_placed = sem("bias_placed")
        idx_staged = sem("idx_staged")
        key_staged = sem("key_staged")
        gathered = [sem(f"gathered{u}") for u in range(BODY)]
        transposed = sem("transposed")
        xT_ready = sem("xT_ready")
        y_ready = sem("y_ready")
        squared = sem("squared")
        std_ready = sem("std_ready")
        same_made = sem("same_made")
        picked = sem("picked")
        scat_ready = sem("scat_ready")
        rstd_made = sem("rstd_made")
        z_made = sem("z_made")
        em_made = sem("em_made")
        summed = sem("summed")
        staged = sem("staged")
        scattered = sem("scattered")
        zeroed = [sem(f"zeroed{i}") for i in range(2)]
        raw_f = sem("raw_f")
        turned = sem("turned")
        tabled = sem("tabled")
        redo_ready = sem("redo_ready")
        redo_summed = sem("redo_summed")
        early_loaded = [sem(f"early_loaded{i}") for i in range(XRING)]
        padded = sem("padded")
        dots_made = sem("dots_made")
        gates_made = sem("gates_made")
        unit_loaded = [sem(f"unit_loaded{i}") for i in range(XRING)]
        cnt_step = sem("cnt_step")
        scale_ready = sem("scale_ready")
        mean_made = sem("mean_made")
        n_transposed = sem("n_transposed")
        n_xT = sem("n_xT")
        n_y = sem("n_y")
        n_squared = sem("n_squared")
        n_std = sem("n_std")
        n_rstd = sem("n_rstd")
        n_gate = sem("n_gate")
        n_z = sem("n_z")
        n_h = sem("n_h")
        n_sum = sem("n_sum")
        n_stats = sem("n_stats")
        n_mv = sem("n_mv")
        o_std = sem("o_std")
        o_rstd = sem("o_rstd")
        o_done = sem("o_done")
        stored = [sem(f"stored{i}") for i in range(4)]

        block = ctx.enter_context(nc.Block())

        def await_next(eng, sem, count, due, by):
            if isinstance(count, int):
                eng.wait_ge(sem, count)
            else:
                eng.wait_ge(sem, due)
                eng.reg_add(due, due, by)

        def bodies(eng, body, turn=None):
            for i in range(PEELED):
                body(i, i % 2)
            with eng.Fori(0, (BODIES - PEELED) // 2) as h:
                body(2 * h + PEELED, 1)
                body(2 * h + (PEELED + 1), 0)

        def tail(stages):
            for j in range(PAIRS * BODIES - DELAY, UNITS + PAUSE + DEPTH):
                for step, behind, behind_last in stages:
                    if j - behind < UNITS - PAIRS:
                        step(j - behind, (j - behind) % XRING)
                    if UNITS - PAIRS <= j - PAUSE - behind_last < UNITS:
                        step(j - PAUSE - behind_last, (j - PAUSE - behind_last) % XRING)

        def once_more(eng, unit, prepare=None, finish=None):
            eng.wait_ge(redo_ready, 6)
            flag = eng.value_load(redo[0:1, 0:1])
            with eng.If(flag > 0):
                if prepare:
                    prepare()
                with eng.Fori(0, GROUPS // 2) as h:
                    for a in range(2):
                        for k in range(PAIRS):
                            s = (PAIRS * (GROUPS + a) + k) % XRING
                            unit(2 * PAIRS * h + (UNITS + PAIRS * a + k), s, 2 * h + a)
                for k in range(PAIRS):
                    unit(2 * UNITS - PAIRS + k, (2 * UNITS - PAIRS + k) % XRING, GROUPS - 1)
                if finish:
                    finish()

        def there(n):
            return not isinstance(n, int) or 0 <= n < UNITS

        def reused(n, ring):
            return not isinstance(n, int) or n >= ring

        def filled_to(n, slot, ring, by):
            return by // ring * (n - slot) + by

        def unit_rows(a, base, kk):
            return a[bass.ds(base, GN), :].rearrange("(p c h) n -> p c (h n)", c=PAIRS, h=UT)[:, kk, :]

        @block.sync
        def _(sp):
            zview = table.rearrange("(c p r) n -> c p (r n)", c=ZC, r=ZROWS)

            def zero(c):
                if c >= 2:
                    sp.wait_ge(zeroed[c % 2], 16 * (c // 2))
                sp.dma_start(zview[ZC - 1 - c, :, :], zeros[:, :]).then_inc(zeroed[c % 2], 16)
            sp.wait_ge(filled, 1)
            zero(0)
            sp.wait_ge(padded, 2)
            for t, a in ((src_raw, src), (dst_raw, dst)):
                sp.dma_start(t[0:BODIES - 1, :], a[0:E - REST].rearrange("(b e) -> b e", e=BE)).then_inc(loaded_idx, 16)
                sp.dma_start(t[BODIES - 1:BODIES, 0:REST], a[E - REST:E].rearrange("(b e) -> b e", b=1)).then_inc(loaded_idx, 16)
            sp.wait_ge(padded, 3)
            sp.dma_start(raw3[0:BODIES - 1, 2, :], edge_w[0:E - REST].rearrange("(b e) -> b e", e=BE)).then_inc(loaded_idx, 16)
            sp.dma_start(raw3[BODIES - 1:BODIES, 2, 0:REST], edge_w[E - REST:E].rearrange("(b e) -> b e", b=1)).then_inc(loaded_idx, 16)

            def base_of(m):
                if isinstance(m, int):
                    return max(N - GN * (m + 1), 0)
                return sp.snap(m * -GN + (N - GN))

            def load_early(n, q, base):
                if reused(n, XRING):
                    sp.wait_ge(dots_made, UT * (n - 7))
                sp.dma_start(x_early[:, q, :, :].rearrange("p t n -> p (t n)"), unit_rows(x, base, q % PAIRS)).then_inc(early_loaded[q], 16)

            def load(n, q, table_base, base, scattered_to=None):
                if reused(n, XRING):
                    sp.wait_ge(n_sum, n - 7)
                sp.dma_start(xg[:, q, :, :].rearrange("p t n -> p (t n)"), unit_rows(x, base, q % PAIRS)).then_inc(unit_loaded[q], 16)
                if q % PAIRS == 0 and scattered_to is not None:
                    sp.wait_ge(scattered, scattered_to)
                sp.dma_start(tg[:, q, :, :].rearrange("p t n -> p (t n)"), unit_rows(table, table_base, q % PAIRS)).then_inc(unit_loaded[q], 16)

            def last_stores(n):
                for c in range(n - 4, n):
                    sp.wait_ge(stored[c % 4], filled_to(c, c % 4, 4, 16))

            def store(n, q, last, base):
                sp.wait_ge(o_done, n + 1)
                if last and q % PAIRS == 0:
                    last_stores(n)
                sp.dma_start(unit_rows(out, base, q % PAIRS),
                             og[:, q % 4, :, :].rearrange("p t n -> p (t n)")).then_inc(stored[q % 4], 16)

            for n in range(XRING):
                load_early(n, n, base_of(n // PAIRS))
            for c in range(1, ZC):
                zero(c)
            sp.wait_ge(redo_ready, 6)
            table_row = sp.alloc_register("table_row")
            sp.reg_mov(table_row, sp.value_load(redo[0:1, 1:2], min_val=0, max_val=SPACE))
            table_step = sp.value_load(redo[0:1, 2:3], min_val=0, max_val=GN)
            table_last = sp.value_load(redo[0:1, 3:4], min_val=0, max_val=SPACE)

            def body(i, a):
                bases = [base_of(i + 1), base_of(i - 2), base_of(i - 4), base_of(i - 5)]
                for k in range(PAIRS):
                    s = PAIRS * i + k
                    q = PAIRS * a + k
                    if not isinstance(s, int) or PAIRS <= s < UNITS - PAIRS:
                        load_early(s + PAIRS, (q + PAIRS) % XRING, bases[0])
                    if there(s - DELAY):
                        if k == 0 and not (isinstance(i, int) and i == 2):
                            sp.reg_sub(table_row, table_row, table_step)
                        load(s - DELAY, q, sp.snap(table_row), bases[1], 16 * BODY * (i - 1))
                    if there(s - DELAY - 9):
                        store(s - DELAY - 9, (q - 9) % XRING, False, bases[3 if k == 0 else 2])
            for i in range(PEELED):
                body(i, i % 2)
            with sp.Fori(0, (BODIES - PEELED) // 2 - 1) as h:
                body(2 * h + PEELED, 1)
                body(2 * h + (PEELED + 1), 0)
            for i in range(BODIES - 2, BODIES):
                body(i, i % 2)

            def load_step(n, q):
                if n == UNITS - 2 * PAIRS:
                    sp.reg_sub(table_row, table_row, table_step)
                load(n, q, table_last if n >= UNITS - PAIRS else sp.snap(table_row), base_of(n // PAIRS), 16 * BODY * (n // PAIRS + 1))

            def store_step(n, q):
                store(n, q, n >= UNITS - PAIRS, base_of(n // PAIRS))
            tail([(load_step, 0, -PAUSE), (store_step, 9, 5)])
            last_stores(UNITS)

            def unit(n, q, m):
                if q % PAIRS == 0:
                    again[0] = base_of(m)
                load(n, q, again[0], again[0])
                store(n, q, isinstance(m, int), again[0])
            again = [None]
            once_more(sp, unit, finish=lambda: last_stores(2 * UNITS))

        @block.gpsimd
        def _(pool):
            slot_used = pool.alloc_register("slot_used")
            before = pool.alloc_register("before")
            pool.reg_mov(slot_used, BODY * PEELED - BODY + 1)
            pool.reg_mov(before, 16 * (BODY * PEELED - LAG))
            nc.gpsimd.memset(src_raw[:, :], 0).then_inc(padded, 1)
            nc.gpsimd.memset(dst_raw[:, :], N + P - 1).then_inc(padded, 1)
            nc.gpsimd.memset(raw3[:, 2, :], 0.0).then_inc(padded, 1)
            nc.gpsimd.memset(reverse[:, :], 0.0).then_inc(consts, 1)
            nc.gpsimd.memset(ident[:, :], 0.0).then_inc(consts, 1)
            nc.gpsimd.memset(order[:, :], 1.0).then_inc(consts, 1)
            pool.wait_ge(consts, 3)
            nc.gpsimd.affine_select(out=reverse[:, :], in_=reverse[:, :], compare_op=ALU.not_equal, fill=1.0,
                                    base=1 - BODIES, pattern=[[1, BODIES]], channel_multiplier=1).then_inc(consts, 1)
            nc.gpsimd.affine_select(out=ident[:, :], in_=ident[:, :], compare_op=ALU.not_equal, fill=1.0,
                                    base=0, pattern=[[-1, P]], channel_multiplier=1).then_inc(consts, 1)
            nc.gpsimd.affine_select(out=order[:, :], in_=order[:, :], compare_op=ALU.is_ge, fill=LATER,
                                    base=0, pattern=[[1, P]], channel_multiplier=-1).then_inc(consts, 1)
            nc.gpsimd.iota(spare_row[:, :], pattern=[[0, 1]], base=N, channel_multiplier=1,
                           allow_small_or_imprecise_dtypes=True).then_inc(consts, 1)
            nc.gpsimd.iota(bound_t[:, :].rearrange("p (m u) -> p m u", u=BODY), pattern=[[-GN, BODIES], [0, BODY]],
                           base=N, channel_multiplier=0, allow_small_or_imprecise_dtypes=True).then_inc(consts, 1)

            def gather(i, u):
                first = isinstance(i, int) and i == 0
                if u % 4 == 0:
                    pool.wait_ge(idx_staged, 2 * i + (u // 4 + 1))
                if not first:
                    await_next(pool, transposed, BODY * i + (u - BODY + 1), slot_used, 1)
                for j, idx in ((0, src_i), (1, dst_i)):
                    nc.gpsimd.indirect_dma_start(
                        rows[:, u, j, :], None, x, bass.IndirectOffsetOnAxis(ap=idx[:, u:u + 1], axis=0)
                    ).then_inc(gathered[u], 16)

            def scatter(i, u):
                first = isinstance(i, int) and i == 0 and u == 0
                if first:
                    pool.wait_ge(redo_ready, 6)
                    needs = [pool.alloc_register(f"need{c}") for c in range(2)]
                    for c, need in enumerate(needs):
                        pool.reg_mov(need, pool.value_load(redo[0:1, 4 + c:5 + c], min_val=16, max_val=16 * ZC // 2))
                pool.wait_ge(staged, PAIRS * i + (u // 2 + 1))
                pool.wait_ge(scat_ready, 2 * (PAIRS * i + (u // 2 + 1)))
                if first:
                    for z, need in zip(zeroed, needs):
                        pool.wait_ge(z, need)
                else:
                    if isinstance(i, int) and i == ZBODIES and u == 0:
                        for z in zeroed:
                            pool.wait_ge(z, 16 * ZC // 2)
                    await_next(pool, scattered, 16 * (BODY * i + u), before, 16)
                nc.gpsimd.indirect_dma_start(
                    table, bass.IndirectOffsetOnAxis(ap=scat_i[:, u:u + 1], axis=0), stage[:, u, :], None,
                    compute_op=ALU.add).then_inc(scattered, 16)

            def body(i, a):
                for u in range(BODY):
                    if u >= LAG:
                        scatter(i, u - LAG)
                    elif not isinstance(i, int) or i > 0:
                        scatter(i - 1, u - LAG + BODY)
                    gather(i, u)
            bodies(pool, body)
            for u in range(BODY - LAG, BODY):
                scatter(BODIES - 1, u)

        @block.tensor
        def _(pe):
            pe.wait_ge(consts, 4)
            for c, b in ((1, XTb), (0, Yb), (2, Db)):
                if c == 2:
                    pe.wait_ge(loaded_idx, 96)
                else:
                    pe.wait_ge(raw_f, 2 - c)
                for u in range(BODY):
                    last = nc.tensor.matmul(b[:, u * BODIES:(u + 1) * BODIES], raw3[:, c, u * P:(u + 1) * P],
                                            reverse[:, :], start=True, stop=True)
                last.then_inc(turned, 1)
            pe.wait_ge(setup, 1)
            for c in range(2):
                nc.tensor.matmul(Ab[0:1, 2 * P + c:2 * P + c + 1], worst[:, 2 * c + 1:2 * c + 2], ones_c[:, :],
                                 start=True, stop=True).then_inc(redo_summed, 1)
            pe.wait_ge(consts, 8)
            pe.wait_ge(bias_placed, 96)
            pe.wait_ge(tabled, 3)

            def transposes(i, k, a):
                s = PAIRS * i + k
                first = isinstance(s, int) and s == 0
                if k == 0:
                    pe.wait_ge(key_staged, i + 1)
                if not first:
                    pe.wait_ge(same_made, 2 * s)
                for h in range(2):
                    u = 2 * k + h
                    nc.tensor.transpose(Db[:, h * P:(h + 1) * P], key_s[:, a, u:u + 1].broadcast_to([P, P]), ident[:, :])
                if not first:
                    pe.wait_ge(xT_ready, s)
                for h in range(2):
                    u = 2 * k + h
                    pe.wait_ge(gathered[u], 32 * i + 32)
                    for j in range(2):
                        last = nc.tensor.transpose(XTb[:, (2 * h + j) * P:(2 * h + j + 1) * P], rows[:, u, j, :], ident[:, :])
                    last.then_inc(transposed, 1)

            def products(i, k):
                s = PAIRS * i + k
                b = k % 2
                pe.wait_ge(xT_ready, s + 1)
                if not (isinstance(s, int) and s == 0):
                    pe.wait_ge(z_made, 2 * s)
                for h in range(2):
                    o = Yb[:, h * 2 * H:(h + 1) * 2 * H]
                    nc.tensor.matmul(o, ones3[:, :], bias3_m[:, :], start=True, stop=False)
                    nc.tensor.matmul(o, xT[:, b, 2 * h * P:(2 * h + 1) * P], msg_wg[:, 0, :], start=False, stop=False)
                    last = nc.tensor.matmul(o, xT[:, b, (2 * h + 1) * P:(2 * h + 2) * P], msg_wg[:, 1, :], start=False, stop=True)
                last.then_inc(y_ready, 1)

            def sums(s, b):
                pe.wait_ge(em_made, 2 * s + 2)
                if not isinstance(s, int) or s >= 1:
                    pe.wait_ge(staged, s)
                for h in range(2):
                    q = 2 * b + h
                    last = nc.tensor.matmul(Ab[:, h * P:(h + 1) * P], same[:, q, :], em[:, q, :], start=True, stop=True)
                last.then_inc(summed, 1)

            def unit_transposes(n, q):
                pe.wait_ge(unit_loaded[q], filled_to(n, q, XRING, 32))
                pe.wait_ge(mean_made, n + 1)
                if reused(n, 2):
                    pe.wait_ge(n_xT, n - 1)
                for t in range(UT):
                    nc.tensor.transpose(XTn[q % 2][:, 2 * t * P:(2 * t + 1) * P], xg[:, q, t, :], ident[:, :])
                    last = nc.tensor.transpose(XTn[q % 2][:, (2 * t + 1) * P:(2 * t + 2) * P], mg[:, q % 4, t, :], ident[:, :])
                last.then_inc(n_transposed, 1)

            def unit_products(n, q):
                pe.wait_ge(n_xT, n + 1)
                if reused(n, 2):
                    pe.wait_ge(n_z, n - 1)
                for t in range(UT):
                    o = Yn[q % 2][:, t * 2 * H:(t + 1) * 2 * H]
                    nc.tensor.matmul(o, ones3[:, :], bias3_u[:, :], start=True, stop=False)
                    nc.tensor.matmul(o, nT[:, q % 2, 2 * t, :], upd_wg[:, 0, :], start=False, stop=False)
                    last = nc.tensor.matmul(o, nT[:, q % 2, 2 * t + 1, :], upd_wg[:, 1, :], start=False, stop=True)
                last.then_inc(n_y, 1)

            def body(i, a):
                for k in range(PAIRS):
                    n = PAIRS * i + (k - DELAY - 3)
                    q = (PAIRS * a + k - 3) % XRING
                    transposes(i, k, a)
                    if there(n):
                        unit_transposes(n, q)
                    if not (isinstance(i, int) and i == 0 and k == 0):
                        sums(PAIRS * i + (k - 1), (k - 1) % 2)
                    products(i, k)
                    if there(n):
                        unit_products(n, q)
            bodies(pe, body)
            sums(PAIRS * BODIES - 1, 1)

            def unit(n, q, m=None):
                unit_transposes(n, q)
                unit_products(n, q)

            ahead = PAIRS * BODIES - DELAY - 3
            unit_transposes(ahead, ahead % XRING)
            tail([(unit_transposes, 2, -1), (unit_products, 3, 0)])
            once_more(pe, unit)

        @block.scalar
        def _(act):
            act.dma_start(msg_raw[:, :, :], msg_w.rearrange("(a p) n -> p a n", p=P)).then_inc(loaded_w, 16)
            act.dma_start(upd_raw[:, :, :], upd_w.rearrange("(a p) n -> p a n", p=P)).then_inc(loaded_w, 16)
            act.dma_start(gate_w_b[:, :], gate_w.rearrange("n a -> a n").broadcast_to([P, H])).then_inc(loaded_w, 16)
            for j, (g, b) in enumerate(((msg_g, msg_beta), (upd_g, upd_beta))):
                act.dma_start(gains[:, j, :], g.rearrange("(a n) -> a n", a=1).broadcast_to([P, H])).then_inc(loaded_w, 16)
                act.dma_start(betas[:, j, :], b.rearrange("(a n) -> a n", a=1).broadcast_to([P, H])).then_inc(loaded_w, 16)
            act.dma_start(bias_raw[:, 0, :], msg_b.rearrange("(a n) -> a n", a=1)).then_inc(loaded_w, 16)
            act.dma_start(bias_raw[:, 1, :], upd_b.rearrange("(a n) -> a n", a=1)).then_inc(loaded_w, 16)
            act.dma_start(gate_b_b[:, :], gate_b.rearrange("(a n) -> a n", a=1).broadcast_to([P, 1])).then_inc(loaded_w, 16)
            act.wait_ge(parts_ready, 6)
            for j in range(3):
                act.dma_start(bias3_m[j:j + 1, :], part_m[:, j, :]).then_inc(bias_placed, 16)
                act.dma_start(bias3_u[j:j + 1, :], part_u[:, j, :]).then_inc(bias_placed, 16)
            act.wait_ge(setup, 1)

            def evacuate(i, k):
                s = PAIRS * i + k
                act.wait_ge(transposed, 2 * s + 2)
                if not isinstance(s, int) or s >= 2:
                    act.wait_ge(y_ready, s - 1)
                nc.scalar.activation(xT[:, k % 2, :], XTb[:, :], ACT.Copy).then_inc(xT_ready, 1)

            def variances(i, k):
                s = PAIRS * i + k
                act.wait_ge(y_ready, s + 1)
                if not isinstance(s, int) or s >= 1:
                    act.wait_ge(squared, 2 * s)
                for h in range(2):
                    u = 2 * k + h
                    nc.scalar.activation(junk[:, h, :], Yb[:, h * 2 * H:h * 2 * H + H], ACT.Square,
                                         accum_out=sumsq[:, u:u + 1]).then_inc(squared, 1)
                act.wait_ge(squared, 2 * s + 2)
                nc.scalar.activation(std[:, 2 * k:2 * k + 2], sumsq[:, 2 * k:2 * k + 2], ACT.Sqrt, bias=eps_c[:, :],
                                     scale=1.0 / H).then_inc(std_ready, 1)

            def sums(s, k):
                act.wait_ge(summed, s + 1)
                if not isinstance(s, int) or s >= PAIRS:
                    act.wait_ge(scattered, 32 * s + 16 * (2 - BODY))
                nc.scalar.activation(stage[:, 2 * k:2 * k + 2, 0:H], Ab[:, 0:2 * P].rearrange("p (h n) -> p h n", h=2),
                                     ACT.Copy).then_inc(staged, 1)

            def make_gates(m, a):
                act.wait_ge(dots_made, GT * m + GT)
                nc.scalar.activation(gates[:, bass.ds(GT * m, GT)], dots[:, a, :], ACT.Sigmoid,
                                     bias=gate_b_b[:, :]).then_inc(gates_made, 1)

            def evacuate_unit(n, q):
                act.wait_ge(n_transposed, n + 1)
                if reused(n, 2):
                    act.wait_ge(n_y, n - 1)
                nc.scalar.activation(nT[:, q % 2, :, :].rearrange("p t n -> p (t n)"), XTn[q % 2][:, :], ACT.Copy).then_inc(n_xT, 1)

            def variances_unit(n, q):
                act.wait_ge(n_y, n + 1)
                if reused(n, 4):
                    act.wait_ge(n_std, n - 3)
                if reused(n, 1):
                    act.wait_ge(n_squared, UT * n)
                for t in range(UT):
                    nc.scalar.activation(nsq[:, t, :], Yn[q % 2][:, 2 * t * H:2 * t * H + H], ACT.Square,
                                         accum_out=ss_u[:, q % 4, t:t + 1]).then_inc(n_squared, 1)
                act.wait_ge(n_squared, UT * n + UT)
                if reused(n, 4):
                    act.wait_ge(n_rstd, n - 3)
                nc.scalar.activation(std_u[:, q % 4, :], ss_u[:, q % 4, :], ACT.Sqrt, scale=1.0 / H, bias=eps_c[:, :]).then_inc(n_std, 1)

            def gated(n, q, m):
                act.wait_ge(n_z, n + 1)
                act.wait_ge(n_gate, 2 * m + 2)
                for t in range(UT):
                    c = UT * (q % PAIRS) + t
                    last = nc.scalar.activation(hg[:, q % 4, t, :], hg[:, q % 4, t, :], ACT.Relu,
                                                scale=gate[:, q // PAIRS, c:c + 1])
                last.then_inc(n_h, 1)

            def std_out(n, q):
                act.wait_ge(n_mv, n + 1)
                if reused(n, 4):
                    act.wait_ge(o_rstd, n - 3)
                nc.scalar.activation(std_o[:, q % 4, :], mv[:, q % 4, :, 1], ACT.Sqrt, bias=eps_c[:, :]).then_inc(o_std, 1)

            def body(i, a):
                for k in range(PAIRS):
                    j = PAIRS * i + (k - DELAY)
                    q = PAIRS * a + k
                    evacuate(i, k)
                    if there(j - 5):
                        gated(j - 5, (q - 5) % XRING, i - 4 if k == 0 else i - 3)
                    if k == 1 and not (isinstance(i, int) and i == 0):
                        make_gates(i - 1, 1 - a)
                    if there(j - 3):
                        evacuate_unit(j - 3, (q - 3) % XRING)
                    if not (isinstance(i, int) and i == 0 and k == 0):
                        sums(PAIRS * i + (k - 1), (k - 1) % PAIRS)
                    variances(i, k)
                    if there(j - 7):
                        std_out(j - 7, (q - 7) % XRING)
                    if there(j - 3):
                        variances_unit(j - 3, (q - 3) % XRING)
            bodies(act, body)
            sums(PAIRS * BODIES - 1, PAIRS - 1)
            make_gates(GROUPS - 1, (GROUPS - 1) % 2)

            ahead = PAIRS * BODIES - DELAY - 3
            evacuate_unit(ahead, ahead % XRING)
            tail([(evacuate_unit, 2, -1), (variances_unit, 3, 0), (lambda n, q: gated(n, q, n // PAIRS), 5, 2), (std_out, 7, 3)])

            def unit(n, q, m):
                evacuate_unit(n, q)
                variances_unit(n, q)
                gated(n, q, m + GROUPS)
                std_out(n, q)
            once_more(act, unit)

        @block.vector
        def _(dve):
            stats_made = dve.alloc_register("stats_made")
            dve.reg_mov(stats_made, PAIRS * PEELED - DELAY - 6 + 1)
            done = [0]
            step = setup_step

            def link(ins):
                done[0] += 1
                ins.then_inc(step, 1)
                dve.wait_ge(step, done[0])

            nc.vector.memset(zeros[:, :], 0.0).then_inc(filled, 1)
            link(nc.vector.memset(ones3[:, :], 1.0))
            link(nc.vector.memset(ones_c[:, :], 1.0))
            link(nc.vector.memset(eps_c[:, :], EPS))
            dve.wait_ge(loaded_idx, 96)
            nc.vector.tensor_copy(raw3[:, 1, :], dst_raw[:, :]).then_inc(raw_f, 1)
            nc.vector.tensor_copy(raw3[:, 0, :], src_raw[:, :]).then_inc(raw_f, 1)
            dve.wait_ge(consts, 8)

            def tiles_in_order(b):
                return b[:, 0:TILES].rearrange("p (u m) -> p m u", u=BODY)

            def whole(t):
                return t[:, 0:TILES].rearrange("p (m u) -> p m u", u=BODY)
            for t in (dgat_t, src_t, key_t, w_t, above_t):
                link(nc.vector.memset(t[:, TILES:], 0))
            dve.wait_ge(turned, 1)
            nc.vector.tensor_copy(whole(key_t), tiles_in_order(XTb)).then_inc(tabled, 1)
            dve.wait_ge(tabled, 1)
            link(nc.vector.tensor_scalar(dgat_t[:, 0:TILES], key_t[:, 0:TILES], float(N - 1), None, ALU.min))
            dve.wait_ge(turned, 2)
            nc.vector.tensor_copy(whole(src_t), tiles_in_order(Yb)).then_inc(tabled, 1)
            dve.wait_ge(tabled, 2)

            def stage_idx(i, h):
                lo = BODY * i + 4 * h
                nc.vector.tensor_copy(src_i[:, 4 * h:4 * h + 4], src_t[:, bass.ds(lo, 4)])
                nc.vector.tensor_copy(dst_i[:, 4 * h:4 * h + 4], dgat_t[:, bass.ds(lo, 4)]).then_inc(idx_staged, 1)
            stage_idx(0, 0)
            stage_idx(0, 1)
            dve.wait_ge(turned, 3)
            nc.vector.tensor_copy(whole(w_t), tiles_in_order(Db)).then_inc(tabled, 1)
            link(nc.vector.tensor_scalar(above_t[:, 0:TILES], key_t[:, 0:TILES], spare_row[:, :], None, ALU.subtract))
            link(nc.vector.tensor_tensor(bound_t[:, :], dgat_t[:, 0:TILES], bound_t[:, :], ALU.subtract))
            link(nc.vector.tensor_reduce(worst[:, 0:1], bound_t[:, :], AX.X, ALU.max))
            link(nc.vector.tensor_scalar(worst[:, 1:2], worst[:, 0:1], 0.0, None, ALU.is_ge))
            link(nc.vector.tensor_scalar(bound_t[:, 0:ZBODIES * BODY], dgat_t[:, 0:ZBODIES * BODY], -1.0, None, ALU.mult))
            link(nc.vector.tensor_reduce(worst[:, 2:3], bound_t[:, 0:ZBODIES * BODY], AX.X, ALU.max))
            link(nc.vector.tensor_scalar(worst[:, 3:4], worst[:, 2:3], float(-ZSTART), None, ALU.is_gt))

            dve.wait_ge(loaded_w, 16 * 10)
            for j, (raw, cen) in enumerate(((msg_raw, msg_wg), (upd_raw, upd_wg))):
                for a in range(2):
                    c = 2 * j + a
                    link(nc.vector.tensor_reduce(neg_mean[:, c:c + 1], raw[:, a, :], AX.X, ALU.add))
                    link(nc.vector.tensor_scalar(neg_mean[:, c:c + 1], neg_mean[:, c:c + 1], -1.0 / H, None, ALU.mult))
                    link(nc.vector.tensor_scalar(cen[:, a, 0:H], raw[:, a, :], neg_mean[:, c:c + 1], None, ALU.add))
                    link(nc.vector.tensor_tensor(cen[:, a, H:2 * H], cen[:, a, 0:H], gains[:, j, :], ALU.mult))
            for j, row in enumerate((bias_m, bias_u)):
                c = 4 + j
                link(nc.vector.tensor_reduce(neg_mean[0:1, c:c + 1], bias_raw[:, j, :], AX.X, ALU.add))
                link(nc.vector.tensor_scalar(neg_mean[0:1, c:c + 1], neg_mean[0:1, c:c + 1], -1.0 / H, None, ALU.mult))
                link(nc.vector.tensor_scalar(row[:, 0:H], bias_raw[:, j, :], neg_mean[0:1, c:c + 1], None, ALU.add))
                link(nc.vector.tensor_tensor(row[:, H:2 * H], row[:, 0:H], gains[0:1, j, :], ALU.mult))
            made = 0
            for row, parts in ((bias_m, part_m), (bias_u, part_u)):
                for j in range(3):
                    made = made + 1
                    nc.vector.tensor_copy(parts[:, j, :], row[:, :]).then_inc(parts_ready, 1)
                    dve.wait_ge(parts_ready, made)
                    link(nc.vector.tensor_tensor(row[:, :], row[:, :], parts[:, j, :], ALU.subtract))
            nc.vector.memset(zero_c[:, :], 0.0).then_inc(setup, 1)
            dve.wait_ge(tabled, 3)
            dve.wait_ge(redo_summed, 2)
            link(nc.vector.tensor_scalar(redo_f[:, :], Ab[0:1, 2 * P:2 * P + 2], 1.0, None, ALU.min))
            first0, first1 = 16 * ((ZFIRST + 1) // 2), 16 * (ZFIRST // 2)
            for c, (a, by, plus) in enumerate(((0, 1, 0), (0, SPACE - (N - GN), N - GN), (0, -GN, GN), (0, SPACE, 0),
                                               (1, 8 * ZC - first0, first0), (1, 8 * ZC - first1, first1))):
                nc.vector.tensor_scalar(redo[:, c:c + 1], redo_f[:, a:a + 1], float(by), float(plus), ALU.mult, ALU.add).then_inc(redo_ready, 1)

            def scale(n, q, step):
                if step == 0:
                    dve.wait_ge(unit_loaded[q], filled_to(n, q, XRING, 32))
                    if reused(n, 4):
                        dve.wait_ge(mean_made, n - 3)
                    nc.vector.tensor_scalar(cnt[:, q % 4, 0, :], tg[:, q, :, H], COUNT_EPS, None, ALU.add).then_inc(cnt_step, 1)
                elif step == 1:
                    dve.wait_ge(cnt_step, 2 * n + 1)
                    nc.vector.reciprocal(cnt[:, q % 4, 1, :], cnt[:, q % 4, 0, :]).then_inc(cnt_step, 1)
                else:
                    dve.wait_ge(cnt_step, 2 * n + 2)
                    nc.vector.scalar_tensor_tensor(cnt[:, q % 4, 2, :], tg[:, q, :, H], 0.0, cnt[:, q % 4, 1, :],
                                                   ALU.is_gt, ALU.mult).then_inc(scale_ready, 1)

            def mean(n, q):
                dve.wait_ge(scale_ready, n + 1)
                if reused(n, 4):
                    dve.wait_ge(n_transposed, n - 3)
                for t in range(UT):
                    last = nc.vector.tensor_scalar(mg[:, q % 4, t, :], tg[:, q, t, 0:H], cnt[:, q % 4, 2, t:t + 1], None, ALU.mult)
                last.then_inc(mean_made, 1)

            def group_gates(m, a, again):
                if again or not isinstance(m, int) or m >= 2:
                    dve.wait_ge(n_sum, PAIRS * (m - 1) + (UNITS if again else 0))
                if not again:
                    dve.wait_ge(gates_made, m + 1)
                these = gates[:, bass.ds(GT * m, GT)]
                nc.vector.tensor_copy(gate[:, a, :], these).then_inc(n_gate, 1)
                nc.vector.tensor_scalar(keep[:, a, :], these, -1.0, 2.0, ALU.mult, ALU.add).then_inc(n_gate, 1)

            def root_update(n, q):
                dve.wait_ge(n_std, n + 1)
                if reused(n, 4):
                    dve.wait_ge(n_z, n - 3)
                nc.vector.reciprocal(rstd_u[:, q % 4, :], std_u[:, q % 4, :]).then_inc(n_rstd, 1)

            def norm_update(n, q):
                dve.wait_ge(n_rstd, n + 1)
                if reused(n, 4):
                    dve.wait_ge(n_sum, n - 3)
                for t in range(UT):
                    last = nc.vector.scalar_tensor_tensor(
                        hg[:, q % 4, t, :], Yn[q % 2][:, (2 * t + 1) * H:(2 * t + 2) * H], rstd_u[:, q % 4, t:t + 1],
                        betas[:, 1, :], ALU.mult, ALU.add)
                last.then_inc(n_z, 1)

            def residual(n, q, m):
                dve.wait_ge(n_h, n + 1)
                dve.wait_ge(n_gate, 2 * m + 2)
                if reused(n, 4):
                    dve.wait_ge(o_done, n - 3)
                for t in range(UT):
                    c = UT * (q % PAIRS) + t
                    last = nc.vector.scalar_tensor_tensor(
                        yg[:, q % 4, t, :], xg[:, q, t, :], keep[:, q // PAIRS, c:c + 1], hg[:, q % 4, t, :], ALU.mult, ALU.add)
                last.then_inc(n_sum, 1)

            def moments(n, q):
                if reused(n, 2):
                    dve.wait_ge(n_mv, n - 1)
                dve.wait_ge(n_sum, n + 1)
                for t in range(UT):
                    last = nc.vector.bn_stats(stats[:, q % 2, t, :], yg[:, q % 4, t, :])
                last.then_inc(n_stats, 1)

            def aggregate(n, q):
                if reused(n, 4):
                    dve.wait_ge(o_done, n - 3)
                await_next(dve, n_stats, n + 1, stats_made, 1)
                for t in range(UT):
                    last = nc.vector.bn_aggr(mv[:, q % 4, t, :], stats[:, q % 2, t, :])
                last.then_inc(n_mv, 1)

            def root_out(n, q):
                dve.wait_ge(o_std, n + 1)
                if reused(n, 4):
                    dve.wait_ge(o_done, n - 3)
                nc.vector.reciprocal(rstd_o[:, q % 4, :], std_o[:, q % 4, :]).then_inc(o_rstd, 1)

            def norm_out(n, q):
                dve.wait_ge(o_rstd, n + 1)
                if reused(n, 4):
                    dve.wait_ge(stored[q % 4], filled_to(n - 4, q % 4, 4, 16))
                for t in range(UT):
                    last = nc.vector.tensor_scalar(og[:, q % 4, t, :], yg[:, q % 4, t, :], mv[:, q % 4, t, 0:1],
                                                   rstd_o[:, q % 4, t:t + 1], ALU.subtract, ALU.mult)
                last.then_inc(o_done, 1)

            def gate_dots(m, a, k):
                dve.wait_ge(early_loaded[PAIRS * a + k], filled_to(PAIRS * m + k, PAIRS * a + k, XRING, 16))
                if k == 0:
                    if not isinstance(m, int) or m >= 2:
                        dve.wait_ge(gates_made, m - 1)
                    if not isinstance(m, int) or m >= 1:
                        dve.wait_ge(dots_made, GT * m)
                for t in (2 * k, 2 * k + 1):
                    nc.vector.scalar_tensor_tensor(dot_junk[:, t, :], x_early[:, PAIRS * a + k, t - 2 * k, :], 1.0, gate_w_b[:, :], ALU.mult, ALU.mult,
                                                   accum_out=dots[:, a, t:t + 1]).then_inc(dots_made, 1)

            def stage_keys(i, a):
                if not isinstance(i, int) or i >= 2:
                    dve.wait_ge(em_made, BODY * (i - 1))
                    dve.wait_ge(scat_ready, BODY * (i - 1))
                lo = BODY * i
                nc.vector.tensor_copy(above_s[:, a, :], above_t[:, bass.ds(lo, BODY)])
                nc.vector.tensor_copy(w_s[:, a, :], w_t[:, bass.ds(lo, BODY)])
                nc.vector.tensor_copy(key_s[:, a, :], key_t[:, bass.ds(lo, BODY)]).then_inc(key_staged, 1)
            stage_keys(0, 0)

            def body(i, a):
                for k in range(PAIRS):
                    s = PAIRS * i + k
                    j = PAIRS * i + (k - DELAY)
                    q = PAIRS * a + k
                    b = k % 2
                    pr = slice(2 * k, 2 * k + 2)
                    if k == 0:
                        dve.wait_ge(key_staged, i + 1)
                        if not isinstance(i, int) or i >= 3:
                            group_gates(i - 3, 1 - a, False)
                    dve.wait_ge(transposed, 2 * s + 2)
                    if not isinstance(s, int) or s >= 2:
                        dve.wait_ge(summed, s - 1)
                    for h in range(2):
                        u = 2 * k + h
                        nc.vector.scalar_tensor_tensor(
                            same[:, 2 * b + h, :], Db[:, h * P:(h + 1) * P], key_s[:, a, u:u + 1], order[:, :],
                            ALU.is_equal, ALU.mult, accum_out=dup[:, u:u + 1]).then_inc(same_made, 1)
                    if k % 2 == 1:
                        stage_idx(i + 1, k // 2)
                    if k == 2:
                        stage_keys(i + 1, 1 - a)
                    if there(j - 1):
                        scale(j - 1, (q - 1) % XRING, 0)
                    if there(j - 6):
                        residual(j - 6, (q - 6) % XRING, i - 4 if k <= 1 else i - 3)
                    if there(j - 1):
                        scale(j - 1, (q - 1) % XRING, 1)
                    dve.wait_ge(same_made, 2 * s + 2)
                    nc.vector.scalar_tensor_tensor(pick[:, pr], dup[:, pr], 2.0, above_s[:, a, pr], ALU.is_lt, ALU.mult).then_inc(picked, 1)
                    if there(j - 6):
                        moments(j - 6, (q - 6) % XRING)
                    if there(j - 1):
                        scale(j - 1, (q - 1) % XRING, 2)
                    dve.wait_ge(picked, s + 1)
                    if not isinstance(i, int) or i >= 1:
                        dve.wait_ge(scattered, 32 * s + 16 * (2 - BODY))
                    nc.vector.tensor_scalar(scat_i[:, pr], pick[:, pr], spare_row[:, :], None, ALU.add).then_inc(scat_ready, 1)
                    nc.vector.tensor_scalar(stage[:, pr, H], dup[:, pr], 1 / LATER, 1 - 1 / LATER, ALU.mult, ALU.add).then_inc(scat_ready, 1)
                    if there(j - 6):
                        aggregate(j - 6, (q - 6) % XRING)
                    if there(j - 4):
                        root_update(j - 4, (q - 4) % XRING)
                    if there(j - 1):
                        mean(j - 1, (q - 1) % XRING)
                    if there(j - 4):
                        norm_update(j - 4, (q - 4) % XRING)
                    if there(j - 8):
                        root_out(j - 8, (q - 8) % XRING)
                    dve.wait_ge(std_ready, s + 1)
                    nc.vector.reciprocal(rstd[:, pr], std[:, pr]).then_inc(rstd_made, 1)
                    dve.wait_ge(rstd_made, s + 1)
                    for h in range(2):
                        u = 2 * k + h
                        nc.vector.scalar_tensor_tensor(
                            z[:, 2 * b + h, :], Yb[:, h * 2 * H + H:(h + 1) * 2 * H], rstd[:, u:u + 1], betas[:, 0, :],
                            ALU.mult, ALU.add).then_inc(z_made, 1)
                    for h in range(2):
                        u = 2 * k + h
                        dve.wait_ge(z_made, 2 * s + (h + 1))
                        nc.vector.tensor_scalar(em[:, 2 * b + h, :], z[:, 2 * b + h, :], 0.0, w_s[:, a, u:u + 1],
                                                ALU.max, ALU.mult).then_inc(em_made, 1)
                    if there(j - 8):
                        norm_out(j - 8, (q - 8) % XRING)
                    gate_dots(i, a, k)
            bodies(dve, body)

            def gates_and_root(n, q):
                if q % PAIRS == 0:
                    group_gates(n // PAIRS, q // PAIRS, False)
                root_update(n, q)
            tail([(lambda n, q: scale(n, q, 0), 1, -1), (lambda n, q: residual(n, q, n // PAIRS), 6, 3),
                  (lambda n, q: scale(n, q, 1), 1, -1), (moments, 6, 3), (lambda n, q: scale(n, q, 2), 1, -1),
                  (gates_and_root, 4, 1), (aggregate, 6, 3), (mean, 1, -1), (norm_update, 4, 1),
                  (root_out, 8, 4), (norm_out, 8, 4)])

            def unit(n, q, m):
                for step in range(3):
                    scale(n, q, step)
                mean(n, q)
                if q % PAIRS == 0:
                    group_gates(m, q // PAIRS, True)
                root_update(n, q)
                norm_update(n, q)
                residual(n, q, m + GROUPS)
                moments(n, q)
                aggregate(n, q)
                root_out(n, q)
                norm_out(n, q)
            once_more(dve, unit, prepare=lambda: dve.reg_mov(stats_made, UNITS + 1))


_INS = ["x", "src", "dst", "edge_weight", "L0_gnn_msg_w", "L0_gnn_msg_b", "L0_gnn_msg_g", "L0_gnn_msg_beta",
        "L0_gnn_upd_w", "L0_gnn_upd_b", "L0_gnn_upd_g", "L0_gnn_upd_beta", "L0_gnn_gate_w", "L0_gnn_gate_b"]


def kernel(**inputs):
    import numpy as _np
    import concourse.bacc as _bacc
    from concourse import mybir as _mybir
    from concourse.bass_utils import run_bass_kernel_spmd as _run

    nc = _bacc.Bacc("TRN2", target_bir_lowering=False, num_devices=1)
    arrays, args = {}, []
    for name in _INS:
        a = _np.ascontiguousarray(inputs[name])
        arrays[f"in_{name}_dram"] = a
        args.append(nc.dram_tensor(f"in_{name}_dram", a.shape, _mybir.dt.from_np(a.dtype), kind="ExternalInput").ap())
    args.append(nc.dram_tensor("out_0_dram", inputs["x"].shape, _mybir.dt.float32, kind="ExternalOutput").ap())
    build(nc, *args)
    r = _run(nc, [arrays], core_ids=[0])
    return r.results[0]["out_0_dram"]
```
